# Optimizing a Trainium2 kernel written in Bass

```python
import numpy as np
import jax
import jax.numpy as jnp

def _softmax(x, axis=-1):
    return jax.nn.softmax(x, axis=axis)

def _gelu(x):
    return jax.nn.gelu(x, approximate=True)

def _silu(x):
    return jax.nn.silu(x)

def _sigmoid(x):
    return jax.nn.sigmoid(x)

def _layernorm(x, axis=-1, eps=1e-05):
    m = jnp.mean(x, axis=axis, keepdims=True)
    v = jnp.var(x, axis=axis, keepdims=True)
    return (x - m) / jnp.sqrt(v + eps)

def _scatter_add(tgt, idx, src, axis=0):
    return tgt.at[idx].add(src)

def _segment_sum(src, seg, n):
    return jax.ops.segment_sum(src, seg, n)
kernel_name = 'mk_decoder_preln_d1_seqx_r8_85ac7c'

def setup_inputs(seed: int=0):
    np.random.seed(seed)
    _w = jnp.asarray

    def _rec_inputs():
        import jax
        import jax.numpy as jnp
        _rk = jax.random.key(seed)
        x = -0.0002928 + 1 * jax.random.normal(jax.random.fold_in(_rk, 1), (4, 256, 128), jnp.float32)
        _lenS = 256 - jax.random.randint(jax.random.fold_in(_rk, 7), (4,), 0, max(1, 256 // 4) + 1, jnp.int32)
        _lenS2 = 1601 - jax.random.randint(jax.random.fold_in(_rk, 8), (4,), 0, max(1, 1601 // 4) + 1, jnp.int32)
        _ctx_1024P = jax.random.normal(jax.random.fold_in(_rk, 11), (4, 16, 128), jnp.float32)
        _ctx_1024c = jax.random.dirichlet(jax.random.fold_in(_rk, 511), 0.3 * jnp.ones((16,), jnp.float32), (4, 1601))
        _ctx_1024t = jnp.einsum('bsk,bkd->bsd', _ctx_1024c, _ctx_1024P)
        _ctx_1024t = _ctx_1024t * jax.lax.rsqrt(jnp.mean(jnp.square(_ctx_1024t)) + 1e-12) * 0.953939
        ctx_1024 = -1.39393e-06 + 0.999914 * (_ctx_1024t + 0.3 * jax.random.normal(jax.random.fold_in(_rk, 611), (4, 1601, 128), jnp.float32))
        _validS = jnp.arange(256)[None, :] < _lenS[:, None]
        _validS2 = jnp.arange(1601)[None, :] < _lenS2[:, None]
        _causal = jnp.tril(jnp.ones((256, 256), dtype=bool))
        mask_Bx1xSxS2_ff0 = jnp.where(jnp.ones((4, 1, 256, 1601), dtype=bool), 0.0, -1000000000.0).astype(jnp.float32)
        return (x, ctx_1024, mask_Bx1xSxS2_ff0)
    x, ctx_1024, mask_Bx1xSxS2_ff0 = _rec_inputs()

    def _L0_attn_setup():
        import jax, jax.numpy as jnp
        import numpy as np
        CLIP_VAL = 8
        FRACTION_BITS = 12
        SCALE = float(2 ** FRACTION_BITS)
        EPS = 1.0 / SCALE
        HEADS = 16
        DIM_HEAD = 64

        def make_fxp(x):
            c = CLIP_VAL - EPS
            x = jnp.clip(x, -c, c)
            return jnp.trunc(x * SCALE) / SCALE
        key = jax.random.key(seed)
        k1, k2, k3, k4 = jax.random.split(key, 4)
        B, N, D = (4, 256, 128)
        inner = HEADS * DIM_HEAD
        x = jax.random.normal(k1, (B, N, D), dtype=jnp.float32)
        w_qkv = jax.random.normal(k2, (3 * inner, D), dtype=jnp.float32) * D ** (-0.5)
        w_proj = jax.random.normal(k3, (D, inner), dtype=jnp.float32) * inner ** (-0.5)
        b_proj = jax.random.normal(k4, (D,), dtype=jnp.float32) * 0.01
        return {'x': x, 'w_qkv': w_qkv, 'w_proj': w_proj, 'b_proj': b_proj}
    _L0_attn_all = _L0_attn_setup()
    _L0_attn_in = {k: v for k, v in _L0_attn_all.items() if k in ('w_qkv', 'w_proj', 'b_proj')}
    del _L0_attn_all

    def _L0_xattn_setup():
        import jax, jax.numpy as jnp
        import numpy as np
        HIDDEN = 128
        HEADS = 16
        N, T1, T2 = (2, 256, 256)

        def _split_heads(x):
            n, t, e = x.shape
            return x.reshape(n, t, HEADS, e // HEADS).transpose(0, 2, 1, 3)
        key = jax.random.key(seed)
        k1, k2, k3, k4 = jax.random.split(key, 4)
        q = jax.random.normal(k1, (N, T1, HIDDEN), dtype=jnp.float32)
        encoder_k = jax.random.normal(k2, (N, T2, HIDDEN), dtype=jnp.float32)
        encoder_v = jax.random.normal(k3, (N, T2, HIDDEN), dtype=jnp.float32)
        encoder_attention_mask = jnp.zeros((N, 1, T2, T2), dtype=jnp.float32)
        wo_w = jax.random.normal(k4, (HIDDEN, HIDDEN), dtype=jnp.float32) * (1.0 / np.sqrt(HIDDEN))
        wo_b = jnp.zeros((HIDDEN,), dtype=jnp.float32)
        return {'q': q, 'encoder_k': encoder_k, 'encoder_v': encoder_v, 'encoder_attention_mask': encoder_attention_mask, 'wo_w': wo_w, 'wo_b': wo_b}
    _L0_xattn_all = _L0_xattn_setup()
    _L0_xattn_in = {k: v for k, v in _L0_xattn_all.items() if k in ('wo_w', 'wo_b')}
    del _L0_xattn_all

    def _L0_ffn_setup():
        import jax, jax.numpy as jnp
        import numpy as np
        E, H, F, K = (8, 128, 256, 2)
        B, S = (2, 256)
        key = jax.random.key(seed)
        ks = jax.random.split(key, 8)

        def w(k, shape, fan_in):
            return jax.random.normal(k, shape, jnp.float32) / np.float32(np.sqrt(fan_in))
        return {'x': jax.random.normal(ks[0], (B, S, H), jnp.float32), 'Wgate': w(ks[1], (H, E), H), 'bgate': jnp.zeros((E,), jnp.float32), 'W1': w(ks[2], (E, H, F), H), 'b1': jnp.zeros((E, F), jnp.float32), 'W2': w(ks[3], (E, H, F), H), 'b2': jnp.zeros((E, F), jnp.float32), 'Wg': w(ks[4], (E, F, F), F), 'bg': jnp.zeros((E, F), jnp.float32), 'Wl': w(ks[5], (E, F, F), F), 'bl': jnp.zeros((E, F), jnp.float32), 'W3': w(ks[6], (E, F, H), F), 'b3': jnp.zeros((E, H), jnp.float32)}
    _L0_ffn_all = _L0_ffn_setup()
    _L0_ffn_in = {k: v for k, v in _L0_ffn_all.items() if k in ('Wgate', 'bgate', 'W1', 'b1', 'W2', 'b2', 'Wg', 'bg', 'Wl', 'bl', 'W3', 'b3')}
    del _L0_ffn_all
    return {'x': x, 'ctx_1024': ctx_1024, 'mask_Bx1xSxS2_ff0': mask_Bx1xSxS2_ff0, 'L0_attn_w_qkv': _L0_attn_in['w_qkv'], 'L0_attn_w_proj': _L0_attn_in['w_proj'], 'L0_attn_b_proj': _L0_attn_in['b_proj'], 'L0_xattn_wo_w': _L0_xattn_in['wo_w'], 'L0_xattn_wo_b': _L0_xattn_in['wo_b'], 'L0_ffn_Wgate': _L0_ffn_in['Wgate'], 'L0_ffn_bgate': _L0_ffn_in['bgate'], 'L0_ffn_W1': _L0_ffn_in['W1'], 'L0_ffn_b1': _L0_ffn_in['b1'], 'L0_ffn_W2': _L0_ffn_in['W2'], 'L0_ffn_b2': _L0_ffn_in['b2'], 'L0_ffn_Wg': _L0_ffn_in['Wg'], 'L0_ffn_bg': _L0_ffn_in['bg'], 'L0_ffn_Wl': _L0_ffn_in['Wl'], 'L0_ffn_bl': _L0_ffn_in['bl'], 'L0_ffn_W3': _L0_ffn_in['W3'], 'L0_ffn_b3': _L0_ffn_in['b3']}

def reference(x, ctx_1024, mask_Bx1xSxS2_ff0, L0_attn_w_qkv, L0_attn_w_proj, L0_attn_b_proj, L0_xattn_wo_w, L0_xattn_wo_b, L0_ffn_Wgate, L0_ffn_bgate, L0_ffn_W1, L0_ffn_b1, L0_ffn_W2, L0_ffn_b2, L0_ffn_Wg, L0_ffn_bg, L0_ffn_Wl, L0_ffn_bl, L0_ffn_W3, L0_ffn_b3):
    import jax
    import jax.numpy as jnp

    def _L0_attn_ref(x, w_qkv, w_proj, b_proj):
        import jax, jax.numpy as jnp
        import numpy as np
        CLIP_VAL = 8
        FRACTION_BITS = 12
        SCALE = float(2 ** FRACTION_BITS)
        EPS = 1.0 / SCALE
        HEADS = 16
        DIM_HEAD = 64

        def make_fxp(x):
            c = CLIP_VAL - EPS
            x = jnp.clip(x, -c, c)
            return jnp.trunc(x * SCALE) / SCALE
        B, N, D = x.shape
        h, d = (HEADS, DIM_HEAD)
        scale = d ** (-0.5)
        qkv = jnp.einsum('bnd,ed->bne', x, w_qkv)
        q, k, v = jnp.split(qkv, 3, axis=-1)
        tohd = lambda t: t.reshape(B, N, h, d).transpose(0, 2, 1, 3)
        q, k, v = (make_fxp(tohd(q)), make_fxp(tohd(k)), make_fxp(tohd(v)))
        dots = make_fxp(jnp.einsum('bhnd,bhmd->bhnm', q, k) * scale)
        attn = make_fxp(jax.nn.softmax(dots, axis=-1))
        attn = make_fxp(attn)
        out = make_fxp(jnp.einsum('bhnm,bhmd->bhnd', attn, v))
        out = out.transpose(0, 2, 1, 3).reshape(B, N, h * d)
        out = make_fxp(jnp.einsum('bne,de->bnd', out, w_proj) + b_proj)
        out = make_fxp(out)
        return out

    def _L0_xattn_ref(q, encoder_k, encoder_v, encoder_attention_mask, wo_w, wo_b):
        import jax, jax.numpy as jnp
        import numpy as np
        HIDDEN = 128
        HEADS = 16
        N, T1, T2 = (2, 256, 256)

        def _split_heads(x):
            n, t, e = x.shape
            return x.reshape(n, t, HEADS, e // HEADS).transpose(0, 2, 1, 3)
        qh = _split_heads(q)
        kh = _split_heads(encoder_k)
        vh = _split_heads(encoder_v)
        scores = jnp.einsum('bhqd,bhkd->bhqk', qh, kh) + encoder_attention_mask
        weights = jax.nn.softmax(scores, axis=-1)
        ctx = jnp.einsum('bhqk,bhkd->bhqd', weights, vh)
        ctx = ctx.transpose(0, 2, 1, 3).reshape(q.shape[0], q.shape[1], -1)
        return jax.nn.relu(ctx @ wo_w.T + wo_b)

    def _L0_ffn_ref(x, Wgate, bgate, W1, b1, W2, b2, Wg, bg, Wl, bl, W3, b3):
        import jax, jax.numpy as jnp
        import numpy as np
        E, H, F, K = (8, 128, 256, 2)
        B, S = (2, 256)
        gout = x @ Wgate + bgate
        topv, topi = jax.lax.top_k(gout, K)
        topw = jax.nn.softmax(topv, axis=-1)
        combine = jnp.sum(jax.nn.one_hot(topi, E, dtype=x.dtype) * topw[..., None], axis=-2)
        x1 = jnp.einsum('bsh,ehf->bsef', x, W1) + b1
        x2 = jnp.einsum('bsh,ehf->bsef', x, W2) + b2
        z = x1 * x2
        g = jnp.einsum('bsef,efg->bseg', z, Wg) + bg
        o = g * jax.nn.sigmoid(g) * (jnp.einsum('bsef,efg->bseg', z, Wl) + bl)
        y = jnp.einsum('bsef,efh->bseh', o, W3) + b3
        return jnp.einsum('bse,bseh->bsh', combine, y)
    x = x + _L0_attn_ref(_layernorm(x, axis=-1), L0_attn_w_qkv, L0_attn_w_proj, L0_attn_b_proj)
    x = x + _L0_xattn_ref(_layernorm(x, axis=-1), ctx_1024, ctx_1024, mask_Bx1xSxS2_ff0, L0_xattn_wo_w, L0_xattn_wo_b)
    x = x + _L0_ffn_ref(_layernorm(x, axis=-1), L0_ffn_Wgate, L0_ffn_bgate, L0_ffn_W1, L0_ffn_b1, L0_ffn_W2, L0_ffn_b2, L0_ffn_Wg, L0_ffn_bg, L0_ffn_Wl, L0_ffn_bl, L0_ffn_W3, L0_ffn_b3)
    return x

_drawn_inputs = setup_inputs


def setup_inputs(seed=0):
    import zlib

    import numpy as np

    out = dict(_drawn_inputs(seed))
    spreads = {'L0_xattn_wo_b': (0.0, 0.1),
     'L0_ffn_bgate': (0.0, 0.1),
     'L0_ffn_b1': (0.0, 0.1),
     'L0_ffn_b2': (0.0, 0.1),
     'L0_ffn_bg': (0.0, 0.1),
     'L0_ffn_bl': (0.0, 0.1),
     'L0_ffn_b3': (0.0, 0.1)}
    factors = {}
    for name, (base, spread) in spreads.items():
        noise = np.random.default_rng([zlib.crc32(name.encode()), seed]).standard_normal(out[name].shape)
        drawn = base * np.exp(spread * noise) if base else spread * noise
        out[name] = jnp.asarray(drawn.astype(out[name].dtype))
    for name, factor in factors.items():
        out[name] = (out[name] * factor).astype(out[name].dtype)
    return out
```

```python
import concourse.bass as bass
from concourse import mybir
from contextlib import ExitStack

F32 = mybir.dt.float32
BF16 = mybir.dt.bfloat16
I16 = mybir.dt.int16
U32 = mybir.dt.uint32
ALU = mybir.AluOpType
ACT = mybir.ActivationFunctionType

B, S, D = 4, 256, 128
T = B * S
NT = T // 128
S2 = 1601
KT = (S2 + 127) // 128
KFULL = S2 // 128
KTAIL = S2 - KFULL * 128
H, DH = 16, 64
HP = H // 2
XD = D // H
HG = H // 4
NE, FF = 8, 256
NG = 2 * HG

FXP = 4096.0
NUDGE = 1.0 + 2.0 ** -22
LN_EPS = 1e-5
MAGIC = 1.5 * 2.0 ** 23

CHUNKS = ((0, 1024), (1024, S2 - 1024))
DVE_TILES = (1, 4, 6, 9, 11)
TILE_CUTS = (0, 3, 6, 9, KT)


class Chain:

    def __init__(self, eng, sem):
        self.eng, self.sem, self.base, self.n = eng, sem, 0, 0

    def step(self, ins):
        self.n += 1
        ins.then_inc(self.sem, 1)
        self.eng.wait_ge(self.sem, self.base + self.n)

    def repetition(self, start, i, steps):
        self.base, self.n = start + i * steps, 0

    def after(self, start, repetitions, steps):
        assert self.n == steps, (self.n, steps)
        self.base, self.n = start + repetitions * steps, 0


def wait(eng, semaphore, value):
    if not isinstance(value, int) or value > 0:
        eng.wait_ge(semaphore, value)


def settle(eng, tally, i):
    if not isinstance(i, int):
        eng.sem_inc(tally, 1)


def repeat(eng, count, body):
    body(0)
    with eng.Fori(1, count - 1) as i:
        body(i)
    body(count - 1)


def decoder_layer(nc, x, ctx_in, mask, w_qkv, w_proj, b_proj, wo_w, wo_b, Wgate, bgate,
                  W1, b1, W2, b2, Wg, bg, Wl, bl, W3, b3, out):
    stack = ExitStack()
    with stack:
        def sb(name, shape, dt=F32):
            return stack.enter_context(nc.sbuf_tensor(name, shape, dt))

        def sem(name):
            return stack.enter_context(nc.semaphore(name))

        ident = sb("ident", [128, 128])
        x_in = sb("x_in", [128, NT, D])
        x1 = sb("x1", [128, NT, D])
        acc = x_in
        xn = sb("xn", [128, NT, D])
        xnT = sb("xnT", [128, T])
        stats = sb("stats", [128, NT, 6])
        meanvar = sb("meanvar", [128, NT, 2])
        var_eps = sb("var_eps", [128, NT])
        std = sb("std", [128, NT])
        rstd = sb("rstd", [128, NT])
        wnat = sb("wnat", [128, 3, D])
        wT = sb("wT", [128, 3 * 128])
        woT = sb("woT", [128, D])
        bproj_bc = sb("bproj_bc", [128, D])
        bproj_fx = sb("bproj_fx", [128, D])
        wob_bc = sb("wob_bc", [128, D])
        bgate_bc = sb("bgate_bc", [128, NE])
        wgate = sb("wgate", [128, NE])
        bias_nat = sb("bias_nat", [64, 128])
        bias_T = sb("bias_T", [128, 64])
        b3_sb = sb("b3_sb", [NE, D])
        esum = sb("esum", [128, 2, 4])
        esum4k = sb("esum4k", [128, 4])
        rnorm = sb("rnorm", [128, 4])
        o16 = sb("o16", [128, S], I16)
        nmax = sb("nmax", [128, 2, 4, 2])
        psum_x = sb("psum_x", [128, 2, H])
        rsum_x = sb("rsum_x", [128, H])
        xoT = sb("xoT", [128, HG * 128])
        cnat = sb("cnat", [128, D])
        cT = sb("cT", [128, 128])
        xo = sb("xo", [128, D])
        gate = sb("gate", [128, NT, NE])
        gtop = sb("gtop", [128, NT, 8])
        gidx = sb("gidx", [128, NT, 8], U32)
        gidf = sb("gidf", [128, NT, 8])
        gw = sb("gw", [128, NT, 4])
        iota_e = sb("iota_e", [128, NE])
        pick = sb("pick", [128, 2, NT, NE])
        comb = sb("comb", [128, NE, NT])
        combT = sb("combT", [NE, NT, 128])
        qstack = sb("qstack", [128, H, S], BF16)
        mask_sb = sb("mask_sb", [128, 2, S2])
        v_cur = sb("v_cur", [128, KT, D])
        v_next = sb("v_next", [128, KT, D])
        pT = sb("pT", [128, 4, 512])
        wpT = pT[:, 0:2, :].rearrange("p u k -> p (u k)").rearrange("p (h d) -> p h d", h=HP)

        region_k = sb("region_k", [128, 8 * S2])
        kstack = region_k[:, :].bitcast(BF16).rearrange("p (h k) -> p h k", h=H)
        ctxT = region_k[:, 0:4 * S2].rearrange("p (u k) -> p u k", u=4)
        kparts = region_k[:, 4 * S2:7 * S2].bitcast(BF16).rearrange("p (u i k) -> p u i k", u=2, i=3)

        region_p = sb("region_p", [128, 8 * S2])
        prob = region_p[:, :].rearrange("p (s k) -> p s k", s=8)
        at = 0

        def cut(region, size):
            nonlocal at
            at += size
            return region[:, at - size:at]

        qf = cut(region_p, T)
        kf = cut(region_p, T)
        vf = cut(region_p, T).rearrange("p (t e) -> p t e", t=NT)
        qkv16 = cut(region_p, 3 * T // 2).bitcast(I16).rearrange("p (c t) -> p c t", c=3)
        dot16 = cut(region_p, T).bitcast(I16).rearrange("p (u k) -> p u k", u=2)
        dotf = cut(region_p, T).bitcast(I16).rearrange("p (u k) -> p u k", u=2)
        expd = cut(region_p, 2 * T).rearrange("p (u k) -> p u k", u=2)
        attn_h = cut(region_p, 2 * T).rearrange("p (u k) -> p u k", u=2)
        attn = expd
        attnT = cut(region_p, T)
        assert at <= 8 * S2
        at = 0
        x1s = cut(region_p, 2 * 512).rearrange("p (f t) -> p f t", f=2)
        zed = cut(region_p, 4 * 512).rearrange("p (u f t) -> p u f t", u=2, f=2)
        silu = cut(region_p, 2 * 512).rearrange("p (f t) -> p f t", f=2)
        ogl = cut(region_p, 4 * 512).rearrange("p (u f t) -> p u f t", u=2, f=2)

        region_g = sb("region_g", [128, HP * T])
        oT = region_g[:, :].rearrange("p (h t) -> p h t", h=HP)
        at = 0
        w1_sb = cut(region_g, 2 * FF).rearrange("p (u f) -> p u f", u=2)
        w2_sb = cut(region_g, 2 * FF).rearrange("p (u f) -> p u f", u=2)
        wg_sb = cut(region_g, 4 * FF).rearrange("p (u k f) -> p u k f", u=2, k=2)
        wl_sb = cut(region_g, 4 * FF).rearrange("p (u k f) -> p u k f", u=2, k=2)
        w3_sb = cut(region_g, 4 * D).rearrange("p (u k f) -> p u k f", u=2, k=2)
        xq_T = cut(region_g, T)
        qparts = cut(region_g, 3 * T // 2).bitcast(BF16).rearrange("p (j t) -> p j t", j=3)

        pair = [stack.enter_context(nc.psum_tensor(f"pair{i}", [128, 1024], F32)) for i in range(4)]

        kscr = nc.dram_tensor("kscr", (B, H * XD, 3 * S2), BF16, kind="Internal").ap()
        qscr = nc.dram_tensor("qscr", (3, H * XD, 3, T), BF16, kind="Internal").ap()

        x_loaded = sem("x_loaded")
        small_loaded = sem("small_loaded")
        wproj_loaded = sem("wproj_loaded")
        ctx_loaded = [sem("ctx_loaded_even"), sem("ctx_loaded_odd")]
        wnat_loaded = sem("wnat_loaded")
        mask_loaded = [sem("mask_loaded_0"), sem("mask_loaded_1")]
        kq_loaded = [sem(f"kq_loaded_{g}") for g in range(HG)]
        kscr_written = [sem("kscr_written_even"), sem("kscr_written_odd")]
        qscr_written = sem("qscr_written")
        v_loaded = sem("v_loaded")
        wexp_loaded = [sem("wexp_loaded_0"), sem("wexp_loaded_1")]
        out_written = sem("out_written")

        act_tally = sem("act_tally")
        dve_tally = sem("dve_tally")
        pool_step = sem("pool_step")
        dve_step = sem("dve_step")
        ident_made = sem("ident_made")
        iota_made = sem("iota_made")
        wproj_T = sem("wproj_T")
        wpT_made = sem("wpT_made")
        small_T = sem("small_T")
        smallT_made = sem("smallT_made")
        ctx_T = sem("ctx_T")
        ctxT_made = sem("ctxT_made")
        kparts_made = sem("kparts_made")
        var_made = sem("var_made")
        std_made = sem("std_made")
        xn_made = sem("xn_made")
        xn_T = sem("xn_T")
        xnT_made = sem("xnT_made")

        w_T = sem("w_T")
        wT_made = sem("wT_made")
        qkv_mm = sem("qkv_mm")
        qkv_rounded = sem("qkv_rounded")
        qkv_made = sem("qkv_made")
        dots_mm = sem("dots_mm")
        dots_rounded = sem("dots_rounded")
        dots_made = sem("dots_made")
        exp_made = sem("exp_made")
        attn_made = sem("attn_made")
        attn_T = sem("attn_T")
        attnT_made = sem("attnT_made")
        pv_mm = sem("pv_mm")
        o_rounded = sem("o_rounded")
        o_made = sem("o_made")
        proj_mm = sem("proj_mm")
        x1_made = sem("x1_made")
        qparts_made = sem("qparts_made")

        score_mm = sem("score_mm")
        half_made = sem("half_made")
        masked_made = sem("masked_made")
        prob_made = sem("prob_made")
        prob_T = sem("prob_T")
        pT_act = sem("pT_act")
        pT_dve = sem("pT_dve")
        xpv_mm = sem("xpv_mm")
        v_moved = sem("v_moved")
        xoT_made = sem("xoT_made")
        xo_T = sem("xo_T")
        cnat_made = sem("cnat_made")
        c_T = sem("c_T")
        cT_made = sem("cT_made")
        xproj_mm = sem("xproj_mm")
        xbias_made = sem("xbias_made")
        x2_made = sem("x2_made")

        gate_mm = sem("gate_mm")
        gdiff_made = sem("gdiff_made")
        gexp_made = sem("gexp_made")
        comb_made = sem("comb_made")
        comb_T = sem("comb_T")
        combT_made = sem("combT_made")
        b3_mm = sem("b3_mm")
        acc_made = sem("acc_made")
        up_mm = sem("up_mm")
        x1s_made = sem("x1s_made")
        z_made = sem("z_made")
        gl_mm = sem("gl_mm")
        silu_made = sem("silu_made")
        ogl_made = sem("ogl_made")
        y_mm = sem("y_mm")
        y_added = sem("y_added")

        block = stack.enter_context(nc.Block())

        x_tiles = x.rearrange("b (t p) d -> p (b t) d", p=128)
        out_tiles = out.rearrange("b (t p) d -> p (b t) d", p=128)
        w_rows = w_qkv.rearrange("(c e) d -> e c d", c=3)
        mask_tiles = mask.rearrange("b a (t p) k -> (b a) t p k", p=128)
        CTX_ORDER = (2, 3, 0, 1)
        ctx_home = (v_cur, v_next, v_cur, v_next)

        def ctx_load(eng, b, home, signal):
            eng.dma_start(home[:, 0:KFULL, :],
                          ctx_in[b, 0:KFULL * 128, :].rearrange("(t p) d -> p t d", p=128)).then_inc(signal, 16)
            eng.dma_start(home[0:KTAIL, KFULL, :], ctx_in[b, KFULL * 128:S2, :]).then_inc(signal, 16)

        def expert_load(sp, e, u):
            sp.dma_start(w1_sb[:, u, :], W1[e]).then_inc(wexp_loaded[u], 16)
            sp.dma_start(w2_sb[:, u, :], W2[e]).then_inc(wexp_loaded[u], 16)
            sp.dma_start(wg_sb[:, u, :, :], Wg[e].rearrange("(k p) f -> p k f", p=128)).then_inc(wexp_loaded[u], 16)
            sp.dma_start(wl_sb[:, u, :, :], Wl[e].rearrange("(k p) f -> p k f", p=128)).then_inc(wexp_loaded[u], 16)
            sp.dma_start(w3_sb[:, u, :, :], W3[e].rearrange("(k p) f -> p k f", p=128)).then_inc(wexp_loaded[u], 16)

        @block.sync
        def _(sp):
            sp.dma_start(x_in[:, :, :], x_tiles).then_inc(x_loaded, 16)
            sp.dma_start(wnat[:, :, :], w_rows[0:128, :, :]).then_inc(wnat_loaded, 16)
            sp.dma_start(x1[:, :, :].rearrange("p t d -> p (t d)"), w_proj).then_inc(wproj_loaded, 16)
            for k in range(2):
                ctx_load(sp, CTX_ORDER[k], ctx_home[k], ctx_loaded[k % 2])
            sp.dma_start(xo[:, :], wo_w).then_inc(small_loaded, 16)
            for n, v in enumerate((b1, b2, bg, bl)):
                sp.dma_start(bias_nat[16 * n:16 * n + 16, :], v.rearrange("e (h f) -> (e h) f", h=2)).then_inc(small_loaded, 16)
            sp.dma_start(bproj_bc[:, :], b_proj.partition_broadcast(128)).then_inc(small_loaded, 16)
            sp.dma_start(wob_bc[:, :], wo_b.partition_broadcast(128)).then_inc(small_loaded, 16)
            sp.dma_start(bgate_bc[:, :], bgate.partition_broadcast(128)).then_inc(small_loaded, 16)
            sp.dma_start(wgate[:, :], Wgate).then_inc(small_loaded, 16)
            sp.dma_start(b3_sb[:, :], b3).then_inc(small_loaded, 16)
            for k in range(2, 4):
                sp.wait_ge(ctx_T, 2 * (k - 1))
                ctx_load(sp, CTX_ORDER[k], ctx_home[k], ctx_loaded[k % 2])
            for t in range(2):
                sp.dma_start(mask_sb[:, t, :], mask_tiles[0, t]).then_inc(mask_loaded[t], 16)
            with sp.Fori(1, HP) as hp:
                sp.wait_ge(w_T, hp)
                sp.dma_start(wnat[:, :, :], w_rows[bass.ds(hp * 128, 128), :, :]).then_inc(wnat_loaded, 16)

            def stack_load(b, g):
                ksrc = kscr[b].rearrange("(h d) (i k) -> h (d i) k", h=H, i=3)[4 * g:4 * g + 4]
                for j in range(3):
                    sp.dma_start(kstack[24 * j:24 * j + 24, 4 * g:4 * g + 4, :],
                                 ksrc.rearrange("h r k -> r h k")).then_inc(kq_loaded[g], 16)
                for j in range(3):
                    qsrc = qscr[j].rearrange("(h d) i t -> h (d i) t", h=H)[4 * g:4 * g + 4, :, bass.ds(b * S, S)]
                    sp.dma_start(qstack[24 * j:24 * j + 24, 4 * g:4 * g + 4, :],
                                 qsrc.rearrange("h r t -> r h t")).then_inc(kq_loaded[g], 16)

            for k in range(2):
                sp.wait_ge(kscr_written[k], 16 * B // 2)
            sp.wait_ge(qscr_written, 16 * 3)
            for g in range(HG):
                stack_load(0, g)
            for u in range(2):
                expert_load(sp, u, u)
            with sp.Fori(1, B) as b:
                sp.wait_ge(masked_made, (b - 1) * (NG * 4) + HG * 4)
                sp.dma_start(mask_sb[:, 0, :], mask_tiles[b, 0]).then_inc(mask_loaded[0], 16)
                for g in range(HG):
                    sp.wait_ge(score_mm, (b - 1) * (NG * 8) + (HG + g + 1) * 8)
                    stack_load(b, g)
                sp.wait_ge(masked_made, b * (NG * 4))
                sp.dma_start(mask_sb[:, 1, :], mask_tiles[b, 1]).then_inc(mask_loaded[1], 16)
            with sp.Fori(1, NE // 2) as r:
                for u in range(2):
                    sp.wait_ge(y_mm, 4 * r - 2 + 2 * u)
                    expert_load(sp, 2 * r + u, u)
            sp.wait_ge(y_added, 2 * NE)
            sp.dma_start(out_tiles, acc[:, :, :]).then_inc(out_written, 16)
            sp.wait_ge(out_written, 16)

        @block.gpsimd
        def _(pool):
            chain = Chain(pool, pool_step)
            chain.step(pool.memset(ident[:, :], 0.0))
            pool.affine_select(out=ident[:, :], in_=ident[:, :], compare_op=ALU.not_equal, fill=1.0, base=0,
                               pattern=[[-1, 128]], channel_multiplier=1).then_inc(ident_made, 1)
            pool.iota(iota_e[:, :], pattern=[[1, NE]], base=0, channel_multiplier=0,
                      allow_small_or_imprecise_dtypes=True).then_inc(iota_made, 1)
            for k, b in enumerate(CTX_ORDER):
                pool.wait_ge(ctxT_made, 2 * k + 2)
                if k >= 2:
                    pool.wait_ge(kscr_written[k % 2], 16)
                rest = ctxT[:, k, :]
                for i in range(3):
                    part = kparts[:, k % 2, i, :]
                    if i < 2:
                        chain.step(pool.tensor_copy(part, rest))
                        chain.step(pool.tensor_tensor(rest, rest, part, ALU.subtract))
                    else:
                        pool.tensor_copy(part, rest).then_inc(kparts_made, 1)
                pool.wait_ge(kparts_made, k + 1)
                pool.dma_start(kscr[b], kparts[:, k % 2, :, :].rearrange("p i k -> p (i k)")).then_inc(kscr_written[k % 2], 16)
            pool.wait_ge(qparts_made, 1)
            for j in range(3):
                pool.dma_start(qscr[j], qparts[:, j:j + 1, :].broadcast_to([128, 3, T])).then_inc(qscr_written, 16)
            for b in range(1, B):
                if b == 1:
                    pool.wait_ge(ctx_loaded[1], 64)
                else:
                    pool.wait_ge(v_loaded, 32 * (b - 1))
                for g in range(HG):
                    pool.wait_ge(xpv_mm, KT * (NG * (b - 1) + HG + g + 1))
                    cols = slice(32 * g, 32 * g + 32)
                    pool.tensor_copy(v_cur[:, 0:KFULL, cols], v_next[:, 0:KFULL, cols]).then_inc(v_moved, 1)
                    pool.tensor_copy(v_cur[0:KTAIL, KFULL, cols], v_next[0:KTAIL, KFULL, cols]).then_inc(v_moved, 1)
                if b + 1 < B:
                    pool.wait_ge(v_moved, 8 * b)
                    ctx_load(pool, b + 1, v_next, v_loaded)

        def tile_count(gi, t):
            if t in DVE_TILES:
                return pT_dve, len(DVE_TILES) * gi + DVE_TILES.index(t) + 1
            return pT_act, (KT - len(DVE_TILES)) * gi + t + 1 - sum(d < t for d in DVE_TILES)

        @block.tensor
        def _(pe):
            pe.wait_ge(ident_made, 1)
            pe.wait_ge(wproj_loaded, 16)
            wproj_nat = x1[:, :, :].rearrange("p t d -> p (t d)")
            for n in range(HP):
                last = pe.transpose(pair[3][:, n * 128:(n + 1) * 128], wproj_nat[:, n * 128:(n + 1) * 128], ident[:, :])
            last.then_inc(wproj_T, 1)

            def ctx_transposes(k):
                pe.wait_ge(ctx_loaded[k % 2], 32 * (k // 2 + 1))
                for half, tiles in enumerate((range(0, 8), range(8, KT))):
                    wait(pe, ctxT_made, 2 * (k - 1) + half + 1 if k else 0)
                    for t in tiles:
                        rows = 128 if t < KFULL else KTAIL
                        c = (t % 8) * 128
                        last = pe.transpose(pair[half][:, c:c + rows], ctx_home[k][0:rows, t, :], ident[0:rows, 0:rows])
                    last.then_inc(ctx_T, 1)

            def xn_transposes(n):
                pe.wait_ge(xn_made, n)
                for t in range(NT):
                    last = pe.transpose(pair[2][:, t * 128:(t + 1) * 128], xn[:, t, :], ident[:, :])
                last.then_inc(xn_T, 1)

            ctx_transposes(0)
            ctx_transposes(1)
            xn_transposes(1)
            pe.wait_ge(wpT_made, 1)
            pe.wait_ge(small_loaded, 16 * 10)
            pe.transpose(pair[3][:, 0:128], xo[:, :], ident[:, :])
            pe.transpose(pair[3][:, 128:192], bias_nat[:, :], ident[0:64, 0:64]).then_inc(small_T, 1)
            ctx_transposes(2)
            ctx_transposes(3)

            def weights_T(hp):
                pe.wait_ge(wnat_loaded, 16 * (hp + 1))
                if isinstance(hp, int) and hp == 0:
                    pe.wait_ge(smallT_made, 2)
                for c in range(3):
                    last = pe.transpose(pair[3][:, c * 128:(c + 1) * 128], wnat[:, c, :], ident[:, :])
                last.then_inc(w_T, 1)

            def project_qk(hp, c):
                if c == 0:
                    pe.wait_ge(wT_made, hp + 1)
                    pe.wait_ge(xnT_made, 1)
                wait(pe, qkv_rounded, 3 * hp + c)
                for n in range(2):
                    last = pe.matmul(pair[2][:, n * 512:(n + 1) * 512], wT[:, c * 128:(c + 1) * 128],
                                     xnT[:, n * 512:(n + 1) * 512], start=True, stop=True)
                last.then_inc(qkv_mm, 1)

            def project_v(hp):
                pe.wait_ge(qkv_rounded, 3 * hp + 2)
                for t in range(NT):
                    last = pe.matmul(pair[2][:, t * 128:(t + 1) * 128], xnT[:, t * 128:(t + 1) * 128],
                                     wT[:, 256:384], start=True, stop=True)
                last.then_inc(qkv_mm, 1)

            def dots(hp, b):
                s = B * hp + b
                if b == 0:
                    pe.wait_ge(qkv_made, 3 * hp + 2)
                wait(pe, dots_rounded, s)
                for h in range(2):
                    rows = slice(64 * h, 64 * h + 64)
                    for t in range(2):
                        last = pe.matmul(pair[0][:, h * 512 + t * 256:h * 512 + (t + 1) * 256],
                                         qf[rows, b * S + t * 128:b * S + (t + 1) * 128],
                                         kf[rows, b * S:(b + 1) * S], start=True, stop=True)
                last.then_inc(dots_mm, 1)

            def attn_transposes(hp, b):
                s = B * hp + b
                pe.wait_ge(attn_made, s + 1)
                wait(pe, attnT_made, s)
                for h in range(2):
                    for t in range(2):
                        for k in range(2):
                            c = h * 512 + k * 256 + t * 128
                            a = (2 * h + t) * 256 + k * 128
                            last = pe.transpose(pair[1][:, c:c + 128], attn[:, b % 2, a:a + 128], ident[:, :])
                last.then_inc(attn_T, 1)

            def attn_values(hp, b):
                s = B * hp + b
                if b == 0:
                    pe.wait_ge(qkv_made, 3 * hp + 3)
                pe.wait_ge(attnT_made, s + 1)
                wait(pe, o_rounded, s)
                for k in range(2):
                    for h in range(2):
                        last = pe.matmul(pair[3][64 * h:64 * h + 64, 512:768], vf[:, 2 * b + k, 64 * h:64 * h + 64],
                                         attnT[:, h * 512 + k * 256:h * 512 + (k + 1) * 256],
                                         start=(k == 0), stop=(k == 1))
                last.then_inc(pv_mm, 1)

            weights_T(0)
            project_qk(0, 0)
            project_qk(0, 1)
            project_v(0)
            pe.wait_ge(ctxT_made, 2 * B)

            def head_pair(hp):
                more = not isinstance(hp, int) or hp + 1 < HP
                dots(hp, 0)
                dots(hp, 1)
                for b in range(B):
                    if b == B - 1 and more:
                        weights_T(hp + 1)
                        project_qk(hp + 1, 0)
                        project_qk(hp + 1, 1)
                    attn_transposes(hp, b)
                    if b + 2 < B:
                        dots(hp, b + 2)
                    attn_values(hp, b)
                if more:
                    project_v(hp + 1)

            repeat(pe, HP, head_pair)

            pe.wait_ge(o_made, B * HP)
            for t in range(NT):
                for n in range(HP):
                    last = pe.matmul(pair[0][:, t * 128:(t + 1) * 128], oT[:, n, t * 128:(t + 1) * 128],
                                     wpT[:, n, :], start=(n == 0), stop=(n == HP - 1))
            last.then_inc(proj_mm, 1)
            xn_transposes(2)

            def scores(b, g, j):
                if g == NG:
                    b, g = b + 1, 0
                gi, head, t = NG * b + g, 4 * (g % HG) + j, g // HG
                if j == 0 and t == 0:
                    pe.wait_ge(kq_loaded[g % HG], 96 * (b + 1))
                for c, (k0, size) in enumerate(CHUNKS):
                    wait(pe, (half_made, masked_made)[c], 4 * gi + j)
                    for k in range(0, size, 512):
                        w = min(512, size - k)
                        last = pe.matmul(pair[c][:, k:k + w], qstack[0:72, head, t * 128:(t + 1) * 128],
                                         kstack[0:72, head, k0 + k:k0 + k + w], start=True, stop=True)
                    last.then_inc(score_mm, 1)

            def tile_T(b, g, t):
                gi, n = NG * b + g, KT * g + t
                rows = 128 if t < KFULL else KTAIL
                before = tile_count(gi, t - 2) if t >= 2 else tile_count(gi - 1, t - 2 + KT)
                if t >= 2 or not isinstance(gi, int) or gi > 0:
                    pe.wait_ge(*before)
                for j in range(4):
                    if t == 0:
                        pe.wait_ge(prob_made, 4 * gi + j + 1)
                    c = (n % 2) * 512 + j * 128
                    last = pe.transpose(pair[2][0:rows, c:c + 128], prob[:, (g % 2) * 4 + j, t * 128:t * 128 + rows],
                                        ident[:, :])
                last.then_inc(prob_T, 1)

            def tile_values(b, g, t):
                gi, n, hg = NG * b + g, KT * g + t, g % HG
                rows = 128 if t < KFULL else KTAIL
                if t == 0 and hg == 0:
                    wait(pe, xoT_made, 2 * b + g // HG)
                if t == 0 and g < HG:
                    wait(pe, v_moved, 8 * (b - 1) + 2 * hg + 2 if not isinstance(b, int) or b else 0)
                pe.wait_ge(*tile_count(gi, t))
                for j in range(4):
                    last = pe.matmul(pair[3][32 * j:32 * j + 32, hg * 128:(hg + 1) * 128],
                                     v_cur[0:rows, t, 32 * hg:32 * hg + 32],
                                     pT[0:rows, n % 4, j * 128:(j + 1) * 128], start=(t == 0), stop=(t == KT - 1))
                last.then_inc(xpv_mm, 1)

            def finish_tile(b, t, piece):
                u = 2 * b + t
                if piece == 0:
                    pe.wait_ge(xoT_made, u + 1)
                    wait(pe, xbias_made, u)
                    for g in range(HG):
                        last = pe.transpose(pair[3][:, 512 + g * 128:640 + g * 128], xoT[:, g * 128:(g + 1) * 128], ident[:, :])
                    last.then_inc(xo_T, 1)
                elif piece == 1:
                    pe.wait_ge(cnat_made, u + 1)
                    pe.transpose(pair[3][:, 512:640], cnat[:, :], ident[:, :]).then_inc(c_T, 1)
                else:
                    pe.wait_ge(cT_made, u + 1)
                    pe.matmul(pair[3][:, 640:768], cT[:, :], woT[:, :], start=True, stop=True).then_inc(xproj_mm, 1)

            pe.wait_ge(x1_made, 1)
            for j in range(4):
                scores(0, 0, j)

            def batch(b):
                more = not isinstance(b, int) or b + 1 < B
                for g in range(NG):
                    for j in range(4):
                        if g + 1 < NG or more:
                            scores(b, g + 1, j)
                        for t in range(TILE_CUTS[j], TILE_CUTS[j + 1]):
                            if t == 0:
                                tile_T(b, g, 0)
                            if t + 1 < KT:
                                tile_T(b, g, t + 1)
                            tile_values(b, g, t)
                        if g == HG and j < 3:
                            finish_tile(b, 0, j)
                for piece in range(3):
                    finish_tile(b, 1, piece)

            repeat(pe, B, batch)

            xn_transposes(3)
            pe.wait_ge(xnT_made, 3)
            for t in range(NT):
                last = pe.matmul(pair[3][:, t * NE:(t + 1) * NE], xnT[:, t * 128:(t + 1) * 128], wgate[:, :],
                                 start=True, stop=True)
            last.then_inc(gate_mm, 1)

            def up(m, f, u, c, r):
                if c == 0 and f == 0:
                    pe.wait_ge(wexp_loaded[u], 80 * (r + 1))
                wait(pe, z_made, 2 * m + f - 1)
                for n, w in enumerate((w1_sb, w2_sb)):
                    last = pe.matmul(pair[f][:, n * 512:(n + 1) * 512], w[:, u, f * 128:(f + 1) * 128],
                                     xnT[:, c * 512:(c + 1) * 512], start=True, stop=True)
                last.then_inc(up_mm, 1)

            def gate_linear(m, half, u, c):
                pe.wait_ge(z_made, 2 * m + 2)
                wait(pe, ogl_made, 2 * m + half)
                for n, w in enumerate((wg_sb, wl_sb)):
                    for f in range(2):
                        last = pe.matmul(pair[2][:, n * 512:(n + 1) * 512], w[:, u, f, half * 128:(half + 1) * 128],
                                         zed[:, c, f, :], start=(f == 0), stop=(f == 1))
                last.then_inc(gl_mm, 1)

            def down(m, u, c):
                pe.wait_ge(ogl_made, 2 * m + 2)
                pe.wait_ge(acc_made, 1)
                wait(pe, y_added, m - 1)
                for t in range(4):
                    for f in range(2):
                        last = pe.matmul(pair[3][:, c * 512 + t * 128:c * 512 + (t + 1) * 128],
                                         ogl[:, c, f, t * 128:(t + 1) * 128], w3_sb[:, u, f, :],
                                         start=(f == 0), stop=(f == 1))
                last.then_inc(y_mm, 1)

            up(0, 0, 0, 0, 0)
            up(0, 1, 0, 0, 0)
            pe.wait_ge(comb_made, 1)
            for t in range(NT):
                last = pe.transpose(pair[2][0:NE, t * 128:(t + 1) * 128], comb[:, :, t], ident[:, :])
            last.then_inc(comb_T, 1)
            pe.wait_ge(combT_made, 1)
            for t in range(NT):
                last = pe.matmul(pair[3][:, t * 128:(t + 1) * 128], combT[:, t, :], b3_sb[:, :], start=True, stop=True)
            last.then_inc(b3_mm, 1)

            def two_experts(r):
                more = not isinstance(r, int) or r + 1 < NE // 2
                for u in range(2):
                    for c in range(2):
                        m = 4 * r + 2 * u + c
                        nu, nc_ = (u, 1) if c == 0 else (1 - u, 0)
                        nr = r + 1 if (u, c) == (1, 1) else r
                        for half in range(2):
                            gate_linear(m, half, u, c)
                            if (u, c) != (1, 1) or more:
                                up(m + 1, half, nu, nc_, nr)
                        down(m, u, c)

            repeat(pe, NE // 2, two_experts)

        @block.scalar
        def _(act):
            act.wait_ge(wproj_T, 1)
            act.activation(pT[:, 0:2, :].rearrange("p u k -> p (u k)"), pair[3][:, :], ACT.Copy).then_inc(wpT_made, 1)

            def ctx_move(k):
                for half, size in enumerate((1024, S2 - 1024)):
                    act.wait_ge(ctx_T, 2 * k + half + 1)
                    act.activation(ctxT[:, k, half * 1024:half * 1024 + size], pair[half][:, 0:size],
                                   ACT.Copy).then_inc(ctxT_made, 1)

            def std_of(n):
                act.wait_ge(var_made, n)
                act.activation(std[:, :], var_eps[:, :], ACT.Sqrt).then_inc(std_made, 1)

            def xn_move(n, home):
                act.wait_ge(xn_T, n)
                act.activation(home, pair[2][:, :], ACT.Copy).then_inc(xnT_made, 1)

            std_of(1)
            ctx_move(0)
            ctx_move(1)
            xn_move(1, xnT[:, :])
            act.wait_ge(small_T, 1)
            act.activation(woT[:, :], pair[3][:, 0:128], ACT.Copy).then_inc(smallT_made, 1)
            act.activation(bias_T[:, :], pair[3][:, 128:192], ACT.Copy).then_inc(smallT_made, 1)
            ctx_move(2)
            ctx_move(3)

            def weights_move(hp):
                act.wait_ge(w_T, hp + 1)
                wait(act, qkv_mm, 3 * hp)
                act.activation(wT[:, :], pair[3][:, 0:384], ACT.Copy).then_inc(wT_made, 1)

            def round_qkv(hp, c):
                act.wait_ge(qkv_mm, 3 * hp + c + 1)
                wait(act, qkv_made, 3 * hp + c - 2)
                act.activation(qkv16[:, c, :], pair[2][:, :], ACT.Copy, scale=FXP * NUDGE, bias=-0.5).then_inc(qkv_rounded, 1)

            def round_dots(hp, b):
                s = B * hp + b
                act.wait_ge(dots_mm, s + 1)
                wait(act, dots_made, s - 1)
                act.activation(dot16[:, b % 2, :], pair[0][:, :], ACT.Copy,
                               scale=NUDGE * DH ** -0.5 / FXP, bias=-0.5).then_inc(dots_rounded, 1)

            def exps(hp, b):
                s = B * hp + b
                act.wait_ge(dots_made, s + 1)
                wait(act, attn_T, s - 1)
                for k in range(4):
                    last = act.activation(expd[:, b % 2, k * 256:(k + 1) * 256], dotf[:, b % 2, k * 256:(k + 1) * 256],
                                          ACT.Exp, scale=1.0 / FXP, accum_out=esum[:, b % 2, k:k + 1])
                last.then_inc(exp_made, 1)

            def attn_move(hp, b):
                s = B * hp + b
                act.wait_ge(attn_T, s + 1)
                wait(act, pv_mm, s)
                act.activation(attnT, pair[1][:, :], ACT.Copy).then_inc(attnT_made, 1)

            weights_move(0)
            for c in range(3):
                round_qkv(0, c)

            def head_pair(hp):
                more = not isinstance(hp, int) or hp + 1 < HP
                round_dots(hp, 0)
                for b in range(B):
                    if b + 1 < B:
                        round_dots(hp, b + 1)
                    exps(hp, b)
                    if b >= 1:
                        attn_move(hp, b - 1)
                if more:
                    weights_move(hp + 1)
                    round_qkv(hp + 1, 0)
                    round_qkv(hp + 1, 1)
                attn_move(hp, B - 1)
                if more:
                    round_qkv(hp + 1, 2)

            repeat(act, HP, head_pair)
            std_of(2)
            xn_move(2, xq_T)

            def exp_head(b, g, j):
                if g == NG:
                    b, g = b + 1, 0
                gi, head, t = NG * b + g, 4 * (g % HG) + j, g // HG
                act.wait_ge(masked_made, 4 * gi + j + 1)
                if j == 0 and g % HG == 0:
                    wait(act, cnat_made, 2 * b + t - 1)
                place = prob[:, (g % 2) * 4 + j, :]
                act.activation(place, place, ACT.Exp, scale=-1.0, bias=nmax[:, g % 2, j, 1:2],
                               accum_out=psum_x[:, t, head:head + 1]).then_inc(prob_made, 1)

            def tile_move(b, g, t):
                n = KT * g + t
                rows = 128 if t < KFULL else KTAIL
                act.wait_ge(prob_T, NG * KT * b + n + 1)
                wait(act, xpv_mm, NG * KT * b + n - 3)
                act.activation(pT[0:rows, n % 4, :], pair[2][0:rows, (n % 2) * 512:(n % 2) * 512 + 512],
                               ACT.Copy).then_inc(pT_act, 1)

            def finish_tile(b, t, piece):
                u = 2 * b + t
                if piece == 0:
                    act.wait_ge(xpv_mm, KT * HG * (u + 1))
                    wait(act, xo_T, u)
                    act.activation(xoT[:, :], pair[3][:, 0:512], ACT.Copy).then_inc(xoT_made, 1)
                else:
                    act.wait_ge(c_T, u + 1)
                    wait(act, xproj_mm, u)
                    act.activation(cT[:, :], pair[3][:, 512:640], ACT.Copy).then_inc(cT_made, 1)

            for j in range(4):
                exp_head(0, 0, j)

            def batch(b):
                more = not isinstance(b, int) or b + 1 < B
                for g in range(NG):
                    if g == HG:
                        finish_tile(b, 0, 0)
                    for j in range(4):
                        for t in range(TILE_CUTS[j], TILE_CUTS[j + 1]):
                            if t not in DVE_TILES:
                                tile_move(b, g, t)
                        if g + 1 < NG or more:
                            exp_head(b, g + 1, j)
                        if g == HG and j == 1:
                            finish_tile(b, 0, 1)
                finish_tile(b, 1, 0)
                finish_tile(b, 1, 1)

            repeat(act, B, batch)

            std_of(3)
            xn_move(3, xnT[:, :])
            act.wait_ge(gdiff_made, 1)
            act.activation(gw[:, :, 1], gw[:, :, 0], ACT.Exp).then_inc(gexp_made, 1)

            def up_bias(m, f, e):
                wait(act, z_made, 2 * m + f - 1)
                act.wait_ge(up_mm, 2 * m + f + 1)
                bias = bias_T[:, bass.ds(2 * e + f, 1)]
                settle(act, act_tally, m)
                act.activation(x1s[:, f, :], pair[f][:, 0:512], ACT.Identity,
                               bias=bias).then_inc(x1s_made, 1)

            def gate_silu(m, half, e):
                wait(act, ogl_made, 2 * m + half - 1)
                act.wait_ge(gl_mm, 2 * m + half + 1)
                bias = bias_T[:, bass.ds(32 + 2 * e + half, 1)]
                settle(act, act_tally, m)
                act.activation(silu[:, half, :], pair[2][:, 0:512], ACT.Silu,
                               bias=bias).then_inc(silu_made, 1)

            up_bias(0, 0, 0)
            up_bias(0, 1, 0)
            act.wait_ge(comb_T, 1)
            act.activation(combT[:, :, :].rearrange("e t p -> e (t p)"), pair[2][0:NE, :], ACT.Copy).then_inc(combT_made, 1)

            def two_experts(r):
                more = not isinstance(r, int) or r + 1 < NE // 2
                for u in range(2):
                    for c in range(2):
                        m, e = 4 * r + 2 * u + c, 2 * r + u
                        for half in range(2):
                            gate_silu(m, half, e)
                            if (u, c) != (1, 1) or more:
                                up_bias(m + 1, half, e + c)

            repeat(act, NE // 2, two_experts)

        @block.vector
        def _(dve):
            chain = Chain(dve, dve_step)

            def layer_norm(n, src):
                for t in range(NT):
                    last = dve.bn_stats(stats[:, t, :], src[:, t, :])
                chain.step(last)
                for t in range(NT):
                    last = dve.bn_aggr(meanvar[:, t, :], stats[:, t, :])
                chain.step(last)
                dve.tensor_scalar(var_eps[:, :], meanvar[:, :, 1], LN_EPS, None, ALU.add).then_inc(var_made, 1)
                dve.wait_ge(std_made, n)
                chain.step(dve.reciprocal(rstd[:, :], std[:, :]))
                for t in range(NT):
                    last = dve.tensor_scalar(xn[:, t, :], src[:, t, :], meanvar[:, t, 0:1], rstd[:, t:t + 1],
                                             ALU.subtract, ALU.mult)
                last.then_inc(xn_made, 1)

            def truncate(out_, floor16):
                return dve.scalar_tensor_tensor(out_, floor16, 0.0, floor16, ALU.is_lt, ALU.add)

            dve.wait_ge(x_loaded, 16)
            layer_norm(1, x_in)
            dve.wait_ge(small_loaded, 16 * 10)
            chain.step(dve.tensor_scalar(bproj_fx[:, :], bproj_bc[:, :], FXP, None, ALU.mult))

            def make_qkv(hp, c):
                dve.wait_ge(qkv_rounded, 3 * hp + c + 1)
                if c < 2:
                    wait(dve, dots_mm, B * hp)
                else:
                    wait(dve, pv_mm, B * hp)
                home = (qf, kf, vf)[c]
                src = qkv16[:, c, :] if c < 2 else qkv16[:, c, :].rearrange("p (t e) -> p t e", t=NT)
                truncate(home, src).then_inc(qkv_made, 1)

            def make_dots(hp, b):
                s = B * hp + b
                dve.wait_ge(dots_rounded, s + 1)
                wait(dve, exp_made, s - 1)
                truncate(dotf[:, b % 2, :], dot16[:, b % 2, :]).then_inc(dots_made, 1)

            def make_attn(hp, b):
                s = B * hp + b
                dve.wait_ge(exp_made, s + 1)
                chain.step(dve.tensor_scalar(esum4k[:, :], esum[:, b % 2, :], 1.0 / (FXP * NUDGE), None, ALU.mult))
                chain.step(dve.reciprocal(rnorm[:, :], esum4k[:, :]))
                for k in range(4):
                    last = dve.tensor_scalar(attn_h[:, b % 2, k * 256:(k + 1) * 256], expd[:, b % 2, k * 256:(k + 1) * 256],
                                             rnorm[:, k:k + 1], -0.5, ALU.mult, ALU.add)
                chain.step(last)
                dve.tensor_scalar(attn[:, b % 2, :], attn_h[:, b % 2, :], MAGIC, MAGIC, ALU.add,
                                  ALU.subtract).then_inc(attn_made, 1)

            def make_o(hp, b):
                s = B * hp + b
                wait(dve, o_made, s)
                dve.wait_ge(pv_mm, s + 1)
                dve.tensor_scalar(o16[:, :], pair[3][:, 512:768], NUDGE / FXP, -0.5, ALU.mult, ALU.add).then_inc(o_rounded, 1)
                dve.wait_ge(o_rounded, s + 1)
                home = oT[:, hp, b * S:(b + 1) * S] if isinstance(hp, int) else \
                    region_g[:, bass.ds(hp * T + b * S, S)]
                truncate(home, o16[:, :]).then_inc(o_made, 1)

            for c in range(3):
                make_qkv(0, c)
            start, steps = chain.base + chain.n, 3 * B

            def head_pair(hp):
                chain.repetition(start, hp, steps)
                more = not isinstance(hp, int) or hp + 1 < HP
                make_dots(hp, 0)
                for b in range(B):
                    if b + 1 < B:
                        make_dots(hp, b + 1)
                    make_attn(hp, b)
                    if b >= 1:
                        make_o(hp, b - 1)
                if more:
                    make_qkv(hp + 1, 0)
                    make_qkv(hp + 1, 1)
                make_o(hp, B - 1)
                if more:
                    make_qkv(hp + 1, 2)

            repeat(dve, HP, head_pair)
            chain.after(start, HP, steps)

            dve.wait_ge(proj_mm, 1)
            flat = xn[:, :, :].rearrange("p t d -> p (t d)")
            chain.step(dve.tensor_tensor(xn[:, :, :], pair[0][:, :].rearrange("p (t d) -> p t d", t=NT),
                                         bproj_fx[:, :].unsqueeze(1).broadcast_to([128, NT, D]), ALU.add))
            chain.step(dve.tensor_scalar(qkv16[:, 0, :], flat, NUDGE, -0.5, ALU.mult, ALU.add))
            chain.step(truncate(flat, qkv16[:, 0, :]))
            dve.scalar_tensor_tensor(x1[:, :, :], xn[:, :, :], 1.0 / FXP, x_in[:, :, :], ALU.mult,
                                     ALU.add).then_inc(x1_made, 1)
            dve.wait_ge(x1_made, 1)
            layer_norm(2, x1)
            dve.wait_ge(xnT_made, 2)
            for i in range(3):
                if i < 2:
                    chain.step(dve.tensor_copy(qparts[:, i, :], xq_T))
                    chain.step(dve.tensor_tensor(xq_T, xq_T, qparts[:, i, :], ALU.subtract))
                else:
                    dve.tensor_copy(qparts[:, i, :], xq_T).then_inc(qparts_made, 1)

            def mask_chunk(b, g, j, c):
                if g == NG:
                    b, g = b + 1, 0
                gi, t = NG * b + g, g // HG
                k0, size = CHUNKS[c]
                if c == 0:
                    if j == 0 and g % HG == 0:
                        dve.wait_ge(mask_loaded[t], 16 * (b + 1))
                    wait(dve, prob_T, KT * (gi - 1))
                    first = 3.0e38
                else:
                    dve.wait_ge(half_made, 4 * gi + j + 1)
                    first = nmax[:, g % 2, j, 0:1]
                dve.wait_ge(score_mm, 8 * gi + 2 * j + c + 1)
                settle(dve, dve_tally, b)
                dve.tensor_tensor_reduce(out=prob[:, (g % 2) * 4 + j, k0:k0 + size], in0=pair[c][:, 0:size],
                                         in1=mask_sb[:, t, k0:k0 + size], scale=-1.0, scalar=first,
                                         op0=ALU.add, op1=ALU.min,
                                         accum_out=nmax[:, g % 2, j, c:c + 1]).then_inc((half_made, masked_made)[c], 1)

            def tile_move(b, g, t):
                n = KT * g + t
                rows = 128 if t < KFULL else KTAIL
                dve.wait_ge(prob_T, NG * KT * b + n + 1)
                wait(dve, xpv_mm, NG * KT * b + n - 3)
                dve.tensor_copy(pT[0:rows, n % 4, :], pair[2][0:rows, (n % 2) * 512:(n % 2) * 512 + 512]).then_inc(pT_dve, 1)

            def finish_tile(b, t, piece):
                u = 2 * b + t
                if piece == 0:
                    dve.wait_ge(prob_made, 4 * HG * (u + 1))
                    chain.step(dve.reciprocal(rsum_x[:, :], psum_x[:, t, :]))
                    dve.wait_ge(xo_T, u + 1)
                    wait(dve, c_T, u)
                    for g in range(HG):
                        heads = [pair[3][:, 512 + g * 128 + 40 * j:512 + g * 128 + 40 * j + XD] for j in range(4)]
                        for j in range(4):
                            last = dve.tensor_scalar(cnat[:, 32 * g + 8 * j:32 * g + 8 * j + 8], heads[j],
                                                     rsum_x[:, 4 * g + j:4 * g + j + 1], None, ALU.mult)
                    last.then_inc(cnat_made, 1)
                else:
                    dve.wait_ge(xproj_mm, u + 1)
                    dve.tensor_tensor(xo[:, :], pair[3][:, 640:768], wob_bc[:, :], ALU.add).then_inc(xbias_made, 1)
                    dve.wait_ge(xbias_made, u + 1)
                    tile = slice(u, u + 1) if isinstance(u, int) else bass.ds(u, 1)
                    dve.scalar_tensor_tensor(acc[:, tile, :], xo[:, :].unsqueeze(1), 0.0, x1[:, tile, :], ALU.max,
                                             ALU.add).then_inc(x2_made, 1)

            for j in range(4):
                for c in range(2):
                    mask_chunk(0, 0, j, c)
            start, steps = chain.base + chain.n, 2

            def batch(b):
                chain.repetition(start, b, steps)
                more = not isinstance(b, int) or b + 1 < B
                for g in range(NG):
                    for j in range(4):
                        if g + 1 < NG or more:
                            for c in range(2):
                                mask_chunk(b, g + 1, j, c)
                        for t in range(TILE_CUTS[j], TILE_CUTS[j + 1]):
                            if t in DVE_TILES:
                                tile_move(b, g, t)
                        if g == HG and j == 0:
                            finish_tile(b, 0, 0)
                        if g == HG and j == 3:
                            finish_tile(b, 0, 1)
                finish_tile(b, 1, 0)
                finish_tile(b, 1, 1)

            repeat(dve, B, batch)
            chain.after(start, B, steps)

            dve.wait_ge(x2_made, 2 * B)
            layer_norm(3, acc)
            dve.wait_ge(gate_mm, 1)
            chain.step(dve.tensor_tensor(gate[:, :, :], pair[3][:, 0:NT * NE].rearrange("p (t e) -> p t e", t=NT),
                                         bgate_bc[:, :].unsqueeze(1).broadcast_to([128, NT, NE]), ALU.add))
            for t in range(NT):
                last = dve.max(gtop[:, t, :], gate[:, t, :])
            chain.step(last)
            dve.tensor_tensor(gw[:, :, 0], gtop[:, :, 1], gtop[:, :, 0], ALU.subtract).then_inc(gdiff_made, 1)
            for t in range(NT):
                last = dve.max_index(gidx[:, t, :], gtop[:, t, :], gate[:, t, :])
            chain.step(last)
            chain.step(dve.tensor_copy(gidf[:, :, :], gidx[:, :, :]))
            dve.wait_ge(gexp_made, 1)
            chain.step(dve.tensor_scalar(gw[:, :, 2], gw[:, :, 1], 1.0, None, ALU.add))
            chain.step(dve.reciprocal(gw[:, :, 3], gw[:, :, 2]))
            chain.step(dve.tensor_tensor(gw[:, :, 2], gw[:, :, 1], gw[:, :, 3], ALU.mult))
            dve.wait_ge(iota_made, 1)
            every = [128, NT, NE]
            for k in range(2):
                last = dve.tensor_tensor(pick[:, k, :, :], iota_e[:, :].unsqueeze(1).broadcast_to(every),
                                         gidf[:, :, k:k + 1].broadcast_to(every), ALU.is_equal)
            chain.step(last)
            for k in range(2):
                last = dve.tensor_tensor(pick[:, k, :, :], pick[:, k, :, :],
                                         gw[:, :, 3 - k:4 - k].broadcast_to(every), ALU.mult)
            chain.step(last)
            dve.tensor_tensor(comb[:, :, :].rearrange("p e t -> p t e"), pick[:, 0, :, :], pick[:, 1, :, :],
                              ALU.add).then_inc(comb_made, 1)

            def zed_of(m, f, e, c):
                dve.wait_ge(x1s_made, 2 * m + f + 1)
                wait(dve, gl_mm, 2 * m - 2)
                dve.scalar_tensor_tensor(zed[:, c, f, :], pair[f][:, 512:1024], bias_T[:, bass.ds(16 + 2 * e + f, 1)],
                                         x1s[:, f, :], ALU.add, ALU.mult).then_inc(z_made, 1)

            def ogl_of(m, half, e, c):
                dve.wait_ge(silu_made, 2 * m + half + 1)
                wait(dve, y_mm, m - 1)
                dve.scalar_tensor_tensor(ogl[:, c, half, :], pair[2][:, 512:1024], bias_T[:, bass.ds(48 + 2 * e + half, 1)],
                                         silu[:, half, :], ALU.add, ALU.mult).then_inc(ogl_made, 1)

            def add_expert(m, e, c):
                dve.wait_ge(y_mm, m + 1)
                wait(dve, y_added, m - 1)
                weight = comb[:, :, :].rearrange("p e t -> p (e t)")
                for t in range(4):
                    last = dve.scalar_tensor_tensor(acc[:, 4 * c + t, :], pair[3][:, c * 512 + t * 128:c * 512 + (t + 1) * 128],
                                                    weight[:, bass.ds(e * NT + 4 * c + t, 1)], acc[:, 4 * c + t, :],
                                                    ALU.mult, ALU.add)
                last.then_inc(y_added, 1)

            zed_of(0, 0, 0, 0)
            zed_of(0, 1, 0, 0)
            dve.wait_ge(b3_mm, 1)
            dve.tensor_tensor(acc[:, :, :], acc[:, :, :], pair[3][:, :].rearrange("p (t d) -> p t d", t=NT),
                              ALU.add).then_inc(acc_made, 1)
            dve.wait_ge(acc_made, 1)

            def two_experts(r):
                more = not isinstance(r, int) or r + 1 < NE // 2
                for u in range(2):
                    for c in range(2):
                        m, e = 4 * r + 2 * u + c, 2 * r + u
                        for half in range(2):
                            ogl_of(m, half, e, c)
                            if (u, c) != (1, 1) or more:
                                zed_of(m + 1, half, e + c, 1 - c)
                        add_expert(m, e, c)

            repeat(dve, NE // 2, two_experts)


_INS = ['x', 'ctx_1024', 'mask_Bx1xSxS2_ff0', 'L0_attn_w_qkv', 'L0_attn_w_proj', 'L0_attn_b_proj',
        'L0_xattn_wo_w', 'L0_xattn_wo_b', 'L0_ffn_Wgate', 'L0_ffn_bgate', 'L0_ffn_W1', 'L0_ffn_b1',
        'L0_ffn_W2', 'L0_ffn_b2', 'L0_ffn_Wg', 'L0_ffn_bg', 'L0_ffn_Wl', 'L0_ffn_bl', 'L0_ffn_W3', 'L0_ffn_b3']


def kernel(**inputs):
    import numpy as _np
    import concourse.bacc as _bacc
    from concourse import mybir as _mybir
    from concourse.bass_utils import run_bass_kernel_spmd as _run

    nc = _bacc.Bacc("TRN2", target_bir_lowering=False, num_devices=1)
    arrays, args = {}, []
    for name in _INS:
        a = _np.ascontiguousarray(inputs[name])
        arrays[f"in_{name}"] = a
        args.append(nc.dram_tensor(f"in_{name}", a.shape, _mybir.dt.from_np(a.dtype), kind="ExternalInput").ap())
    out = nc.dram_tensor("out", (4, 256, 128), _mybir.dt.float32, kind="ExternalOutput").ap()
    decoder_layer(nc, *args, out)
    r = _run(nc, [arrays], core_ids=[0])
    return r.results[0]["out"]
```

```python
import concourse.bass as bass
from concourse import mybir
from contextlib import ExitStack

F32 = mybir.dt.float32
BF16 = mybir.dt.bfloat16
I16 = mybir.dt.int16
U32 = mybir.dt.uint32
ALU = mybir.AluOpType
ACT = mybir.ActivationFunctionType
AX = mybir.AxisListType
RMAX = bass.bass_isa.ReduceOp.max

B, S, D = 4, 256, 128
T = B * S
NT = T // 128
S2 = 1601
KT = (S2 + 127) // 128
KFULL = S2 // 128
KTAIL = S2 - KFULL * 128
H, DH = 16, 64
HP = H // 2
XD = D // H
HG = H // 4
NE, FF = 8, 256
NG = 2 * HG

FXP = 4096.0
NUDGE = 1.0 + 2.0 ** -22
LN_EPS = 1e-5
MAGIC = 1.5 * 2.0 ** 23

CHUNKS = ((0, 1024), (1024, S2 - 1024))
AHEAD = 6
SROWS = 72
SHIFT = 96
ONE_BF16_TWICE = 1.0 + 0x3F80 / 2.0 ** 23


class Chain:

    def __init__(self, eng, sem):
        self.eng, self.sem, self.base, self.n = eng, sem, 0, 0

    def step(self, ins):
        self.n += 1
        ins.then_inc(self.sem, 1)
        self.eng.wait_ge(self.sem, self.base + self.n)

    def repetition(self, start, i, steps):
        self.base, self.n = start + i * steps, 0

    def after(self, start, repetitions, steps):
        assert self.n == steps, (self.n, steps)
        self.base, self.n = start + repetitions * steps, 0


def wait(eng, semaphore, value):
    if not isinstance(value, int) or value > 0:
        eng.wait_ge(semaphore, value)


def settle(eng, tally, i):
    if not isinstance(i, int):
        eng.sem_inc(tally, 1)


def repeat(eng, count, body):
    body(0)
    with eng.Fori(1, count - 1) as i:
        body(i)
    body(count - 1)


def decoder_layer(nc, x, ctx_in, mask, w_qkv, w_proj, b_proj, wo_w, wo_b, Wgate, bgate,
                  W1, b1, W2, b2, Wg, bg, Wl, bl, W3, b3, out):
    stack = ExitStack()
    with stack:
        def sb(name, shape, dt=F32):
            return stack.enter_context(nc.sbuf_tensor(name, shape, dt))

        def sem(name):
            return stack.enter_context(nc.semaphore(name))

        ident = sb("ident", [128, 128])
        x_in = sb("x_in", [128, NT, D])
        x1 = sb("x1", [128, NT, D])
        acc = x_in
        xn = sb("xn", [128, NT, D])
        xnT = sb("xnT", [128, T])
        stats = sb("stats", [128, NT, 6])
        meanvar = sb("meanvar", [128, NT, 2])
        var_eps = sb("var_eps", [128, NT])
        std = sb("std", [128, NT])
        rstd = sb("rstd", [128, NT])
        wnat = sb("wnat", [128, 3, D])
        wT = sb("wT", [128, 3 * 128])
        woT = sb("woT", [128, D])
        bproj_bc = sb("bproj_bc", [128, D])
        bproj_fx = sb("bproj_fx", [128, D])
        wob_bc = sb("wob_bc", [128, D])
        bgate_bc = sb("bgate_bc", [128, NE])
        wgate = sb("wgate", [128, NE])
        bias_nat = sb("bias_nat", [64, 128])
        bias_T = sb("bias_T", [128, 64])
        b3_sb = sb("b3_sb", [NE, D])
        esum = sb("esum", [128, 2, 4])
        esum4k = sb("esum4k", [128, 4])
        rnorm = sb("rnorm", [128, 4])
        o16 = sb("o16", [128, S], I16)
        nmax = sb("nmax", [128, 2, 4, 2])
        nparts = sb("nparts", [128, 2, 4, 3], BF16)
        nrest = sb("nrest", [128, 4])
        mask_hi = sb("mask_hi", [128, 2])
        mask_any = sb("mask_any", [128, 2])
        mask_flag = sb("mask_flag", [128, 2])
        identb = sb("identb", [128, 128], BF16)
        rsum_x = sb("rsum_x", [128, H])
        xo = sb("xo", [128, D])
        gate = sb("gate", [128, NT, NE])
        gtop = sb("gtop", [128, NT, 8])
        gidx = sb("gidx", [128, NT, 8], U32)
        gidf = sb("gidf", [128, NT, 8])
        gw = sb("gw", [128, NT, 4])
        iota_e = sb("iota_e", [128, NE])
        pick = sb("pick", [128, 2, NT, NE])
        comb = sb("comb", [128, NE, NT])
        combT = sb("combT", [NE, NT, 128])
        qstack = sb("qstack", [128, H, S], BF16)
        mask_sb = sb("mask_sb", [128, 2, S2])
        v_nat = mask_sb[:, :, :].rearrange("p t k -> p (t k)")[:, 0:KT * D].rearrange("p (t d) -> p t d", t=KT)
        v_next = sb("v_next", [128, KT, D])
        VW = XD + 1
        v_aug = sb("v_aug", [128, KT, H * VW + 32 - VW])
        pT = sb("pT", [128, 4, 512])
        wpT = pT[:, 0:2, :].rearrange("p u k -> p (u k)").rearrange("p (h d) -> p h d", h=HP)

        region_k = sb("region_k", [128, 8 * S2])
        kstack = region_k[:, :].bitcast(BF16).rearrange("p (h k) -> p h k", h=H)
        ctxT = region_k[:, 0:4 * S2].rearrange("p (u k) -> p u k", u=4)
        kparts = region_k[:, 4 * S2:7 * S2].bitcast(BF16).rearrange("p (u i k) -> p u i k", u=2, i=3)

        region_p = sb("region_p", [128, 8 * S2])
        at = 0

        def cut(region, size):
            nonlocal at
            at += size
            return region[:, at - size:at]

        qf = cut(region_p, T)
        kf = cut(region_p, T)
        vf = cut(region_p, T).rearrange("p (t e) -> p t e", t=NT)
        qkv16 = cut(region_p, 3 * T // 2).bitcast(I16).rearrange("p (c t) -> p c t", c=3)
        dot16 = cut(region_p, T).bitcast(I16).rearrange("p (u k) -> p u k", u=2)
        dotf = cut(region_p, T).bitcast(I16).rearrange("p (u k) -> p u k", u=2)
        expd = cut(region_p, 2 * T).rearrange("p (u k) -> p u k", u=2)
        attn_h = cut(region_p, 2 * T).rearrange("p (u k) -> p u k", u=2)
        attn = expd
        attnT = cut(region_p, T)
        assert at <= 8 * S2
        at = 0
        mparts = cut(region_p, 3 * S2).bitcast(BF16).rearrange("p (u i k) -> p u i k", u=2, i=3)
        mrest = cut(region_p, S2)
        unused = [cut(region_p, 1024), cut(region_p, 1024)]
        xoT = cut(region_p, HG * 128)
        cnat = cut(region_p, D)
        cT = cut(region_p, 128)
        assert at <= 8 * S2
        at = 0
        x1s = cut(region_p, 2 * 512).rearrange("p (f t) -> p f t", f=2)
        zed = cut(region_p, 4 * 512).rearrange("p (u f t) -> p u f t", u=2, f=2)
        silu = cut(region_p, 2 * 512).rearrange("p (f t) -> p f t", f=2)
        ogl = cut(region_p, 4 * 512).rearrange("p (u f t) -> p u f t", u=2, f=2)

        region_g = sb("region_g", [128, HP * T])
        oT = region_g[:, :].rearrange("p (h t) -> p h t", h=HP)
        at = 0
        w1_sb = cut(region_g, 2 * FF).rearrange("p (u f) -> p u f", u=2)
        w2_sb = cut(region_g, 2 * FF).rearrange("p (u f) -> p u f", u=2)
        wg_sb = cut(region_g, 4 * FF).rearrange("p (u k f) -> p u k f", u=2, k=2)
        wl_sb = cut(region_g, 4 * FF).rearrange("p (u k f) -> p u k f", u=2, k=2)
        w3_sb = cut(region_g, 4 * D).rearrange("p (u k f) -> p u k f", u=2, k=2)
        xq_T = cut(region_g, T)
        qparts = cut(region_g, 3 * T // 2).bitcast(BF16).rearrange("p (j t) -> p j t", j=3)

        pair = [stack.enter_context(nc.psum_tensor(f"pair{i}", [128, 1024], F32)) for i in range(4)]

        nm_psum = pair[3][:, 512:1024].bitcast(BF16)

        kscr = nc.dram_tensor("kscr", (B, H * XD, 3 * S2), BF16, kind="Internal").ap()
        qscr = nc.dram_tensor("qscr", (3, H * XD, 3, T), BF16, kind="Internal").ap()

        x_loaded = sem("x_loaded")
        small_loaded = sem("small_loaded")
        wproj_loaded = sem("wproj_loaded")
        ctx_loaded = [sem("ctx_loaded_even"), sem("ctx_loaded_odd")]
        wnat_loaded = sem("wnat_loaded")
        mask_loaded = [sem("mask_loaded_0"), sem("mask_loaded_1")]
        kq_loaded = [sem(f"kq_loaded_{g}") for g in range(HG)]
        kscr_written = [sem("kscr_written_even"), sem("kscr_written_odd")]
        qscr_written = sem("qscr_written")
        v_loaded = sem("v_loaded")
        wexp_loaded = [sem("wexp_loaded_0"), sem("wexp_loaded_1")]
        out_written = sem("out_written")

        act_tally = sem("act_tally")
        pe_tally = sem("pe_tally")
        dve_tally = sem("dve_tally")
        pool_step = sem("pool_step")
        dve_step = sem("dve_step")
        ident_made = sem("ident_made")
        iota_made = sem("iota_made")
        wproj_T = sem("wproj_T")
        wpT_made = sem("wpT_made")
        small_T = sem("small_T")
        smallT_made = sem("smallT_made")
        ctx_T = sem("ctx_T")
        ctxT_made = sem("ctxT_made")
        kparts_made = sem("kparts_made")
        var_made = sem("var_made")
        std_made = sem("std_made")
        xn_made = sem("xn_made")
        xn_T = sem("xn_T")
        xnT_made = sem("xnT_made")

        w_T = sem("w_T")
        wT_made = sem("wT_made")
        qkv_mm = sem("qkv_mm")
        qkv_rounded = sem("qkv_rounded")
        qkv_made = sem("qkv_made")
        dots_mm = sem("dots_mm")
        dots_rounded = sem("dots_rounded")
        dots_made = sem("dots_made")
        exp_made = sem("exp_made")
        attn_made = sem("attn_made")
        attn_T = sem("attn_T")
        attnT_made = sem("attnT_made")
        pv_mm = sem("pv_mm")
        o_rounded = sem("o_rounded")
        o_made = sem("o_made")
        proj_mm = sem("proj_mm")
        x1_made = sem("x1_made")
        qparts_made = sem("qparts_made")

        stacks_set = sem("stacks_set")
        score_mm = sem("score_mm")
        half_made = sem("half_made")
        masked_made = sem("masked_made")
        nparts_made = sem("nparts_made")
        nm_T = sem("nm_T")
        nm_moved = sem("nm_moved")
        any_made = sem("any_made")
        flag_made = sem("flag_made")
        mparts_made = sem("mparts_made")
        v0_made = sem("v0_made")
        st_mm = sem("st_mm")
        expt_made = sem("expt_made")
        xpv_mm = sem("xpv_mm")
        v_moved = sem("v_moved")
        xoT_made = sem("xoT_made")
        xo_T = sem("xo_T")
        cnat_made = sem("cnat_made")
        c_T = sem("c_T")
        cT_made = sem("cT_made")
        xproj_mm = sem("xproj_mm")
        xbias_made = sem("xbias_made")
        x2_made = sem("x2_made")

        gate_mm = sem("gate_mm")
        gdiff_made = sem("gdiff_made")
        gexp_made = sem("gexp_made")
        comb_made = sem("comb_made")
        comb_T = sem("comb_T")
        combT_made = sem("combT_made")
        b3_mm = sem("b3_mm")
        acc_made = sem("acc_made")
        up_mm = sem("up_mm")
        x1s_made = sem("x1s_made")
        z_made = sem("z_made")
        gl_mm = sem("gl_mm")
        silu_made = sem("silu_made")
        ogl_made = sem("ogl_made")
        y_mm = sem("y_mm")
        y_added = sem("y_added")

        block = stack.enter_context(nc.Block())

        x_tiles = x.rearrange("b (t p) d -> p (b t) d", p=128)
        out_tiles = out.rearrange("b (t p) d -> p (b t) d", p=128)
        w_rows = w_qkv.rearrange("(c e) d -> e c d", c=3)
        mask_tiles = mask.rearrange("b a (t p) k -> (b a) t p k", p=128)
        CTX_ORDER = (2, 3, 0, 1)
        ctx_home = (v_nat, v_next, v_nat, v_next)

        def ctx_load(eng, b, home, signal):
            eng.dma_start(home[:, 0:KFULL, :],
                          ctx_in[b, 0:KFULL * 128, :].rearrange("(t p) d -> p t d", p=128)).then_inc(signal, 16)
            eng.dma_start(home[0:KTAIL, KFULL, :], ctx_in[b, KFULL * 128:S2, :]).then_inc(signal, 16)

        def expert_load(sp, e, u):
            sp.dma_start(w1_sb[:, u, :], W1[e]).then_inc(wexp_loaded[u], 16)
            sp.dma_start(w2_sb[:, u, :], W2[e]).then_inc(wexp_loaded[u], 16)
            sp.dma_start(wg_sb[:, u, :, :], Wg[e].rearrange("(k p) f -> p k f", p=128)).then_inc(wexp_loaded[u], 16)
            sp.dma_start(wl_sb[:, u, :, :], Wl[e].rearrange("(k p) f -> p k f", p=128)).then_inc(wexp_loaded[u], 16)
            sp.dma_start(w3_sb[:, u, :, :], W3[e].rearrange("(k p) f -> p k f", p=128)).then_inc(wexp_loaded[u], 16)

        @block.sync
        def _(sp):
            sp.dma_start(x_in[:, :, :], x_tiles).then_inc(x_loaded, 16)
            sp.dma_start(wnat[:, :, :], w_rows[0:128, :, :]).then_inc(wnat_loaded, 16)
            sp.dma_start(x1[:, :, :].rearrange("p t d -> p (t d)"), w_proj).then_inc(wproj_loaded, 16)
            for k in range(2):
                ctx_load(sp, CTX_ORDER[k], ctx_home[k], ctx_loaded[k % 2])
            sp.dma_start(xo[:, :], wo_w).then_inc(small_loaded, 16)
            for n, v in enumerate((b1, b2, bg, bl)):
                sp.dma_start(bias_nat[16 * n:16 * n + 16, :], v.rearrange("e (h f) -> (e h) f", h=2)).then_inc(small_loaded, 16)
            sp.dma_start(bproj_bc[:, :], b_proj.partition_broadcast(128)).then_inc(small_loaded, 16)
            sp.dma_start(wob_bc[:, :], wo_b.partition_broadcast(128)).then_inc(small_loaded, 16)
            sp.dma_start(bgate_bc[:, :], bgate.partition_broadcast(128)).then_inc(small_loaded, 16)
            sp.dma_start(wgate[:, :], Wgate).then_inc(small_loaded, 16)
            sp.dma_start(b3_sb[:, :], b3).then_inc(small_loaded, 16)
            for k in range(2, 4):
                sp.wait_ge(ctx_T, 2 * (k - 1))
                ctx_load(sp, CTX_ORDER[k], ctx_home[k], ctx_loaded[k % 2])
            with sp.Fori(1, HP) as hp:
                sp.wait_ge(w_T, hp)
                sp.dma_start(wnat[:, :, :], w_rows[bass.ds(hp * 128, 128), :, :]).then_inc(wnat_loaded, 16)

            def stack_load(b, g):
                ksrc = kscr[b].rearrange("(h d) (i k) -> h (d i) k", h=H, i=3)[4 * g:4 * g + 4]
                for j in range(3):
                    sp.dma_start(kstack[24 * j:24 * j + 24, 4 * g:4 * g + 4, :],
                                 ksrc.rearrange("h r k -> r h k")).then_inc(kq_loaded[g], 16)
                for j in range(3):
                    qsrc = qscr[j].rearrange("(h d) i t -> h (d i) t", h=H)[4 * g:4 * g + 4, :, bass.ds(b * S, S)]
                    sp.dma_start(qstack[24 * j:24 * j + 24, 4 * g:4 * g + 4, :],
                                 qsrc.rearrange("h r t -> r h t")).then_inc(kq_loaded[g], 16)

            sp.wait_ge(v0_made, 2)
            for t in range(2):
                sp.dma_start(mask_sb[:, t, :], mask_tiles[0, t]).then_inc(mask_loaded[t], 16)
            sp.wait_ge(stacks_set, 4)
            sp.wait_ge(qscr_written, 16 * 3)
            for g in range(HG):
                stack_load(0, g)
            for u in range(2):
                expert_load(sp, u, u)

            def mask_load(b, t):
                u = 2 * b + t
                sp.wait_ge(masked_made, 16 * (u - 1))
                sp.wait_ge(mparts_made, u - 1)
                sp.wait_ge(any_made, u - 1)
                sp.dma_start(mask_sb[:, t, :], mask_tiles[b, t]).then_inc(mask_loaded[t], 16)

            with sp.Fori(1, B) as b:
                mask_load(b, 0)
                for g in range(HG):
                    sp.wait_ge(st_mm, KT * (NG * (b - 1) + HG + g + 1))
                    stack_load(b, g)
                    if g == 1:
                        mask_load(b, 1)
            with sp.Fori(1, NE // 2) as r:
                for u in range(2):
                    sp.wait_ge(y_mm, 4 * r - 2 + 2 * u)
                    expert_load(sp, 2 * r + u, u)
            sp.wait_ge(y_added, 2 * NE)
            sp.dma_start(out_tiles, acc[:, :, :]).then_inc(out_written, 16)
            sp.wait_ge(out_written, 16)

        @block.gpsimd
        def _(pool):
            chain = Chain(pool, pool_step)
            chain.step(pool.memset(ident[:, :], 0.0))
            pool.affine_select(out=ident[:, :], in_=ident[:, :], compare_op=ALU.not_equal, fill=1.0, base=0,
                               pattern=[[-1, 128]], channel_multiplier=1).then_inc(ident_made, 1)
            pool.iota(iota_e[:, :], pattern=[[1, NE]], base=0, channel_multiplier=0,
                      allow_small_or_imprecise_dtypes=True).then_inc(iota_made, 1)
            pool.wait_ge(ident_made, 1)
            pool.tensor_copy(identb[:, :], ident[:, :]).then_inc(ident_made, 1)
            pool.wait_ge(ident_made, 2)
            pool.memset(qstack[64:96, :, :].rearrange("p h t -> p (h t)").bitcast(F32), 0.0).then_inc(stacks_set, 1)
            pool.wait_ge(stacks_set, 1)
            chain.step(pool.memset(v_aug[:, :, :], 1.0))

            def split(parts, rest, src, signal):
                for i in range(3):
                    if i < 2:
                        chain.step(pool.tensor_copy(parts[:, i, :], src))
                        chain.step(pool.tensor_tensor(rest, src, parts[:, i, :], ALU.subtract))
                        src = rest
                    else:
                        pool.tensor_copy(parts[:, i, :], src).then_inc(signal, 1)

            def move_values(nat, g, signal):
                for rows, tiles in ((128, slice(0, KFULL)), (KTAIL, slice(KFULL, KT))):
                    dst = v_aug[0:rows, tiles, 4 * VW * g:4 * VW * (g + 1)].rearrange("p t (j c) -> p t j c", j=4)
                    src = nat[0:rows, tiles, 32 * g:32 * g + 32].rearrange("p t (j c) -> p t j c", j=4)
                    pool.tensor_copy(dst[:, :, :, 0:XD], src).then_inc(signal, 1)

            for k, b in enumerate(CTX_ORDER):
                pool.wait_ge(ctxT_made, 2 * k + 2)
                if k >= 2:
                    pool.wait_ge(kscr_written[k % 2], 16)
                split(kparts[:, k % 2, :, :], ctxT[:, k, :], ctxT[:, k, :], kparts_made)
                pool.wait_ge(kparts_made, k + 1)
                pool.dma_start(kscr[b], kparts[:, k % 2, :, :].rearrange("p i k -> p (i k)")).then_inc(kscr_written[k % 2], 16)
            for g in range(HG):
                move_values(v_nat, g, pool_step)
            chain.n += 2 * HG
            pool.wait_ge(pool_step, chain.base + chain.n)
            pool.sem_inc(v0_made, 2)
            for k in range(2):
                pool.wait_ge(kscr_written[k], 32)
            pool.memset(region_k[64:96, :], 0.0).then_inc(stacks_set, 1)
            pool.wait_ge(stacks_set, 2)
            pool.memset(region_k[SHIFT:SHIFT + 3, :], ONE_BF16_TWICE).then_inc(stacks_set, 1)
            pool.wait_ge(stacks_set, 3)
            pool.sem_inc(stacks_set, 1)
            pool.wait_ge(qparts_made, 1)
            for j in range(3):
                pool.dma_start(qscr[j], qparts[:, j:j + 1, :].broadcast_to([128, 3, T])).then_inc(qscr_written, 16)

            def mask_tile(b, t):
                u = 2 * b + t
                pool.wait_ge(any_made, u + 1)
                if u >= 2:
                    pool.wait_ge(st_mm, KT * HG * (u - 1))
                pool.partition_all_reduce(mask_flag[:, t:t + 1], mask_any[:, t:t + 1], 128, RMAX).then_inc(flag_made, 1)
                if u:
                    pool.wait_ge(mparts_made, u)
                split(mparts[:, t, :, :], mrest, mask_sb[:, t, :], mparts_made)

            mask_tile(0, 0)
            mask_tile(0, 1)
            for b in range(1, B):
                mask_tile(b, 0)
                if b == 1:
                    pool.wait_ge(ctx_loaded[1], 64)
                else:
                    pool.wait_ge(v_loaded, 32 * (b - 1))
                for g in range(HG):
                    pool.wait_ge(xpv_mm, KT * (NG * (b - 1) + HG + g + 1))
                    move_values(v_next, g, v_moved)
                if b + 1 < B:
                    pool.wait_ge(v_moved, 8 * b)
                    ctx_load(pool, b + 1, v_next, v_loaded)
                mask_tile(b, 1)

        @block.tensor
        def _(pe):
            pe.wait_ge(ident_made, 1)
            pe.wait_ge(wproj_loaded, 16)
            wproj_nat = x1[:, :, :].rearrange("p t d -> p (t d)")
            for n in range(HP):
                last = pe.transpose(pair[3][:, n * 128:(n + 1) * 128], wproj_nat[:, n * 128:(n + 1) * 128], ident[:, :])
            last.then_inc(wproj_T, 1)

            def ctx_transposes(k, pairs):
                pe.wait_ge(ctx_loaded[k % 2], 32 * (k // 2 + 1))
                for half, tiles in enumerate((range(0, 8), range(8, KT))):
                    if k:
                        pe.wait_ge(ctxT_made, 2 * k + half)
                    for t in tiles:
                        rows = 128 if t < KFULL else KTAIL
                        c = (t % 8) * 128
                        last = pe.transpose(pair[pairs[half]][:, c:c + rows], ctx_home[k][0:rows, t, :], ident[0:rows, 0:rows])
                    last.then_inc(ctx_T, 1)

            def xn_transposes(n):
                pe.wait_ge(xn_made, n)
                for t in range(NT):
                    last = pe.transpose(pair[2][:, t * 128:(t + 1) * 128], xn[:, t, :], ident[:, :])
                last.then_inc(xn_T, 1)

            ctx_transposes(0, (0, 1))
            xn_transposes(1)
            pe.wait_ge(wpT_made, 1)
            pe.wait_ge(small_loaded, 16 * 10)
            pe.transpose(pair[3][:, 0:128], xo[:, :], ident[:, :])
            pe.transpose(pair[3][:, 128:192], bias_nat[:, :], ident[0:64, 0:64]).then_inc(small_T, 1)

            def weights_T(hp):
                pe.wait_ge(wnat_loaded, 16 * (hp + 1))
                if isinstance(hp, int) and hp == 0:
                    pe.wait_ge(smallT_made, 2)
                for c in range(3):
                    last = pe.transpose(pair[3][:, c * 128:(c + 1) * 128], wnat[:, c, :], ident[:, :])
                last.then_inc(w_T, 1)

            def project_qk(hp, c):
                if c == 0:
                    pe.wait_ge(wT_made, hp + 1)
                    pe.wait_ge(xnT_made, 1)
                wait(pe, qkv_rounded, 3 * hp + c)
                if isinstance(hp, int) and hp == 1:
                    pe.wait_ge(ctxT_made, 2 * B)
                for n in range(2):
                    last = pe.matmul(pair[2][:, n * 512:(n + 1) * 512], wT[:, c * 128:(c + 1) * 128],
                                     xnT[:, n * 512:(n + 1) * 512], start=True, stop=True)
                last.then_inc(qkv_mm, 1)

            def project_v(hp):
                pe.wait_ge(qkv_rounded, 3 * hp + 2)
                for t in range(NT):
                    last = pe.matmul(pair[2][:, t * 128:(t + 1) * 128], xnT[:, t * 128:(t + 1) * 128],
                                     wT[:, 256:384], start=True, stop=True)
                last.then_inc(qkv_mm, 1)

            def dots(hp, b):
                s = B * hp + b
                if b == 0:
                    pe.wait_ge(qkv_made, 3 * hp + 2)
                wait(pe, dots_rounded, s)
                for h in range(2):
                    rows = slice(64 * h, 64 * h + 64)
                    for t in range(2):
                        last = pe.matmul(pair[0][:, h * 512 + t * 256:h * 512 + (t + 1) * 256],
                                         qf[rows, b * S + t * 128:b * S + (t + 1) * 128],
                                         kf[rows, b * S:(b + 1) * S], start=True, stop=True)
                last.then_inc(dots_mm, 1)

            def attn_transposes(hp, b):
                s = B * hp + b
                pe.wait_ge(attn_made, s + 1)
                wait(pe, attnT_made, s)
                for h in range(2):
                    for t in range(2):
                        for k in range(2):
                            c = h * 512 + k * 256 + t * 128
                            a = (2 * h + t) * 256 + k * 128
                            last = pe.transpose(pair[1][:, c:c + 128], attn[:, b % 2, a:a + 128], ident[:, :])
                last.then_inc(attn_T, 1)

            def attn_values(hp, b):
                s = B * hp + b
                if b == 0:
                    pe.wait_ge(qkv_made, 3 * hp + 3)
                pe.wait_ge(attnT_made, s + 1)
                wait(pe, o_rounded, s)
                for k in range(2):
                    for h in range(2):
                        last = pe.matmul(pair[3][64 * h:64 * h + 64, 512:768], vf[:, 2 * b + k, 64 * h:64 * h + 64],
                                         attnT[:, h * 512 + k * 256:h * 512 + (k + 1) * 256],
                                         start=(k == 0), stop=(k == 1))
                last.then_inc(pv_mm, 1)

            weights_T(0)
            project_qk(0, 0)
            project_qk(0, 1)
            project_v(0)
            pe.wait_ge(ctxT_made, 2)

            def head_pair(hp):
                more = not isinstance(hp, int) or hp + 1 < HP
                dots(hp, 0)
                dots(hp, 1)
                for b in range(B):
                    if b + 2 < B:
                        dots(hp, b + 2)
                    if b == B - 1 and more:
                        project_qk(hp + 1, 0)
                        project_qk(hp + 1, 1)
                    attn_transposes(hp, b)
                    if b >= 1:
                        attn_values(hp, b - 1)
                    if b == 1 and more:
                        weights_T(hp + 1)
                    if isinstance(hp, int) and hp == 0 and 0 < b + 1 < B:
                        ctx_transposes(b + 1, (2, 2))
                attn_values(hp, B - 1)
                if more:
                    project_v(hp + 1)

            repeat(pe, HP, head_pair)

            pe.wait_ge(o_made, B * HP)
            for t in range(NT):
                for n in range(HP):
                    last = pe.matmul(pair[0][:, t * 128:(t + 1) * 128], oT[:, n, t * 128:(t + 1) * 128],
                                     wpT[:, n, :], start=(n == 0), stop=(n == HP - 1))
            last.then_inc(proj_mm, 1)
            xn_transposes(2)

            def head_of(b, g, j, ahead):
                n = 4 * g + j + ahead
                return (b, n // 4, n % 4) if n < 4 * NG else (b + 1, n // 4 - NG, n % 4)

            def scores(b, g, j):
                gi, head, t = NG * b + g, 4 * (g % HG) + j, g // HG
                if j == 0 and t == 0:
                    pe.wait_ge(kq_loaded[g % HG], 96 * (b + 1))
                for c, (k0, size) in enumerate(CHUNKS):
                    wait(pe, (half_made, masked_made)[c], 4 * gi + j)
                    for k in range(0, size, 512):
                        w = min(512, size - k)
                        last = pe.matmul(pair[c][:, k:k + w], qstack[0:SROWS, head, t * 128:(t + 1) * 128],
                                         kstack[0:SROWS, head, k0 + k:k0 + k + w], start=True, stop=True)
                    last.then_inc(score_mm, 1)

            def maxima_T(b, g):
                gi = NG * b + g
                pe.wait_ge(nparts_made, gi + 1)
                wait(pe, nm_moved, gi)
                for j in range(4):
                    last = pe.transpose(nm_psum[SHIFT:SHIFT + 3, j * 128:(j + 1) * 128], nparts[:, g % 2, j, :],
                                        identb[:, :])
                last.then_inc(nm_T, 1)

            def tile_scores(b, g, t, masked):
                gi, n, hg, q = NG * b + g, KT * g + t, g % HG, g // HG
                rows = 128 if t < KFULL else KTAIL
                if t == 0:
                    pe.wait_ge(nm_moved, gi + 1)
                wait(pe, expt_made, NG * KT * b + n - 1)
                bank = (n % 2) * 512
                for j in range(4):
                    last = pe.matmul(pair[2][0:rows, bank + j * 128:bank + (j + 1) * 128],
                                     kstack[0:SHIFT + 3, 4 * hg + j, t * 128:t * 128 + rows],
                                     qstack[0:SHIFT + 3, 4 * hg + j, q * 128:(q + 1) * 128],
                                     start=(j == 0), stop=True, skip_group_check=True)
                    if j == 0 and masked:
                        for i in range(3):
                            pe.matmul(pair[2][0:rows, bank:bank + 512].rearrange("k (j q) -> k j q", j=4),
                                      mparts[:, q, i, t * 128:t * 128 + rows],
                                      identb[:, :].unsqueeze(1).broadcast_to([128, 4, 128]),
                                      start=False, stop=True, skip_group_check=True)
                last.then_inc(st_mm, 1)

            def tile_values(b, g, t):
                gi, n, hg = NG * b + g, KT * g + t, g % HG
                rows = 128 if t < KFULL else KTAIL
                if t == 0 and hg == 0:
                    wait(pe, xoT_made, 2 * b + g // HG)
                if t == 0 and g < HG:
                    wait(pe, v_moved, 8 * (b - 1) + min(2 * hg + 4, 8))
                pe.wait_ge(expt_made, NG * KT * b + n + 1)
                for j in range(4):
                    c = VW * (4 * hg + j)
                    last = pe.matmul(pair[3][32 * j:32 * j + 32, hg * 128:(hg + 1) * 128],
                                     v_aug[0:rows, t, c:c + 32],
                                     pT[0:rows, n % 4, j * 128:(j + 1) * 128], start=(t == 0), stop=(t == KT - 1))
                last.then_inc(xpv_mm, 1)

            def finish_tile(b, t, piece):
                u = 2 * b + t
                if piece == 0:
                    pe.wait_ge(xoT_made, u + 1)
                    pe.wait_ge(nm_moved, 4 * u + 4)
                    for g in range(HG):
                        last = pe.transpose(pair[3][:, 512 + g * 128:640 + g * 128], xoT[:, g * 128:(g + 1) * 128], ident[:, :])
                    last.then_inc(xo_T, 1)
                elif piece == 1:
                    pe.wait_ge(cnat_made, u + 1)
                    pe.transpose(pair[3][:, 512:640], cnat, ident[:, :]).then_inc(c_T, 1)
                else:
                    pe.wait_ge(cT_made, u + 1)
                    pe.matmul(pair[3][:, 640:768], cT, woT[:, :], start=True, stop=True).then_inc(xproj_mm, 1)

            pe.wait_ge(x1_made, 1)
            for n in range(AHEAD):
                scores(*head_of(0, 0, 0, n))
            maxima_T(0, 0)

            def group(b, g, masked, last_batch):
                def ahead(j):
                    if not last_batch or 4 * g + j + AHEAD < 4 * NG:
                        scores(*head_of(b, g, j, AHEAD))

                last_tile = g // HG - 1
                finish = g % HG == 0 and not (isinstance(b, int) and b == 0 and g == 0)
                unit = (b, 0) if g else (b - 1, 1)
                tile_scores(b, g, 0, masked)
                tile_scores(b, g, 1, masked)
                ahead(0)
                for t in range(KT):
                    if t == KT - 1:
                        ahead(3)
                    tile_values(b, g, t)
                    if t + 2 < KT:
                        tile_scores(b, g, t + 2, masked)
                    if t == 3:
                        ahead(1)
                    if t == 7:
                        ahead(2)
                    if finish and t in (1, 4, 7):
                        finish_tile(*unit, (1, 4, 7).index(t))
                    if t == 9 and (not last_batch or g + 1 < NG):
                        if finish:
                            pe.wait_ge(xbias_made, 2 * unit[0] + unit[1] + 1)
                        maxima_T(*((b, g + 1) if g + 1 < NG else (b + 1, 0)))

            def batch(b):
                last_batch = isinstance(b, int) and b + 1 == B
                for q in range(2):
                    pe.wait_ge(flag_made, 2 * b + q + 1)
                    settle(pe, pe_tally, b)
                    flag = pe.value_load(mask_flag[0:1, q:q + 1].bitcast(U32))
                    with pe.If(flag != 0):
                        pe.wait_ge(mparts_made, 2 * b + q + 1)
                        for g in range(HG * q, HG * (q + 1)):
                            group(b, g, True, last_batch)
                    with pe.Else():
                        for g in range(HG * q, HG * (q + 1)):
                            group(b, g, False, last_batch)

            repeat(pe, B, batch)
            for piece in range(3):
                finish_tile(B - 1, 1, piece)

            xn_transposes(3)
            pe.wait_ge(xnT_made, 3)
            for t in range(NT):
                last = pe.matmul(pair[3][:, t * NE:(t + 1) * NE], xnT[:, t * 128:(t + 1) * 128], wgate[:, :],
                                 start=True, stop=True)
            last.then_inc(gate_mm, 1)

            def up(m, f, u, c, r):
                if c == 0 and f == 0:
                    pe.wait_ge(wexp_loaded[u], 80 * (r + 1))
                wait(pe, z_made, 2 * m + f - 1)
                for n, w in enumerate((w1_sb, w2_sb)):
                    last = pe.matmul(pair[f][:, n * 512:(n + 1) * 512], w[:, u, f * 128:(f + 1) * 128],
                                     xnT[:, c * 512:(c + 1) * 512], start=True, stop=True)
                last.then_inc(up_mm, 1)

            def gate_linear(m, half, u, c):
                pe.wait_ge(z_made, 2 * m + 2)
                wait(pe, ogl_made, 2 * m + half)
                for n, w in enumerate((wg_sb, wl_sb)):
                    for f in range(2):
                        last = pe.matmul(pair[2][:, n * 512:(n + 1) * 512], w[:, u, f, half * 128:(half + 1) * 128],
                                         zed[:, c, f, :], start=(f == 0), stop=(f == 1))
                last.then_inc(gl_mm, 1)

            def down(m, u, c):
                pe.wait_ge(ogl_made, 2 * m + 2)
                pe.wait_ge(acc_made, 1)
                wait(pe, y_added, m - 1)
                for t in range(4):
                    for f in range(2):
                        last = pe.matmul(pair[3][:, c * 512 + t * 128:c * 512 + (t + 1) * 128],
                                         ogl[:, c, f, t * 128:(t + 1) * 128], w3_sb[:, u, f, :],
                                         start=(f == 0), stop=(f == 1))
                last.then_inc(y_mm, 1)

            up(0, 0, 0, 0, 0)
            up(0, 1, 0, 0, 0)
            pe.wait_ge(comb_made, 1)
            for t in range(NT):
                last = pe.transpose(pair[2][0:NE, t * 128:(t + 1) * 128], comb[:, :, t], ident[:, :])
            last.then_inc(comb_T, 1)
            pe.wait_ge(combT_made, 1)
            for t in range(NT):
                last = pe.matmul(pair[3][:, t * 128:(t + 1) * 128], combT[:, t, :], b3_sb[:, :], start=True, stop=True)
            last.then_inc(b3_mm, 1)

            def two_experts(r):
                more = not isinstance(r, int) or r + 1 < NE // 2
                for u in range(2):
                    for c in range(2):
                        m = 4 * r + 2 * u + c
                        nu, nc_ = (u, 1) if c == 0 else (1 - u, 0)
                        nr = r + 1 if (u, c) == (1, 1) else r
                        for half in range(2):
                            gate_linear(m, half, u, c)
                            if (u, c) != (1, 1) or more:
                                up(m + 1, half, nu, nc_, nr)
                        down(m, u, c)

            repeat(pe, NE // 2, two_experts)

        @block.scalar
        def _(act):
            act.wait_ge(wproj_T, 1)
            act.activation(pT[:, 0:2, :].rearrange("p u k -> p (u k)"), pair[3][:, :], ACT.Copy).then_inc(wpT_made, 1)

            def ctx_move(k, pairs):
                for half, size in enumerate((1024, S2 - 1024)):
                    act.wait_ge(ctx_T, 2 * k + half + 1)
                    act.activation(ctxT[:, k, half * 1024:half * 1024 + size], pair[pairs[half]][:, 0:size],
                                   ACT.Copy).then_inc(ctxT_made, 1)

            def std_of(n):
                act.wait_ge(var_made, n)
                act.activation(std[:, :], var_eps[:, :], ACT.Sqrt).then_inc(std_made, 1)

            def xn_move(n, home):
                act.wait_ge(xn_T, n)
                act.activation(home, pair[2][:, :], ACT.Copy).then_inc(xnT_made, 1)

            std_of(1)
            ctx_move(0, (0, 1))
            xn_move(1, xnT[:, :])
            act.wait_ge(small_T, 1)
            act.activation(woT[:, :], pair[3][:, 0:128], ACT.Copy).then_inc(smallT_made, 1)
            act.activation(bias_T[:, :], pair[3][:, 128:192], ACT.Copy).then_inc(smallT_made, 1)

            def weights_move(hp):
                act.wait_ge(w_T, hp + 1)
                wait(act, qkv_mm, 3 * hp)
                act.activation(wT[:, :], pair[3][:, 0:384], ACT.Copy).then_inc(wT_made, 1)

            def round_qkv(hp, c):
                act.wait_ge(qkv_mm, 3 * hp + c + 1)
                wait(act, qkv_made, 3 * hp + c - 2)
                act.activation(qkv16[:, c, :], pair[2][:, :], ACT.Copy, scale=FXP * NUDGE, bias=-0.5).then_inc(qkv_rounded, 1)

            def round_dots(hp, b):
                s = B * hp + b
                act.wait_ge(dots_mm, s + 1)
                wait(act, dots_made, s - 1)
                act.activation(dot16[:, b % 2, :], pair[0][:, :], ACT.Copy,
                               scale=NUDGE * DH ** -0.5 / FXP, bias=-0.5).then_inc(dots_rounded, 1)

            def exps(hp, b):
                s = B * hp + b
                act.wait_ge(dots_made, s + 1)
                wait(act, attn_T, s - 1)
                for k in range(4):
                    last = act.activation(expd[:, b % 2, k * 256:(k + 1) * 256], dotf[:, b % 2, k * 256:(k + 1) * 256],
                                          ACT.Exp, scale=1.0 / FXP, accum_out=esum[:, b % 2, k:k + 1])
                last.then_inc(exp_made, 1)

            def attn_move(hp, b):
                s = B * hp + b
                act.wait_ge(attn_T, s + 1)
                wait(act, pv_mm, s)
                act.activation(attnT, pair[1][:, :], ACT.Copy).then_inc(attnT_made, 1)

            weights_move(0)
            for c in range(3):
                round_qkv(0, c)

            def head_pair(hp):
                more = not isinstance(hp, int) or hp + 1 < HP
                round_dots(hp, 0)
                for b in range(B):
                    if b + 1 < B:
                        round_dots(hp, b + 1)
                    if b == B - 1 and more:
                        weights_move(hp + 1)
                    exps(hp, b)
                    if b >= 1:
                        attn_move(hp, b - 1)
                    if isinstance(hp, int) and hp == 0 and b + 1 < B:
                        ctx_move(b + 1, (2, 2))
                if more:
                    round_qkv(hp + 1, 0)
                    round_qkv(hp + 1, 1)
                attn_move(hp, B - 1)
                if more:
                    round_qkv(hp + 1, 2)

            repeat(act, HP, head_pair)
            std_of(2)
            xn_move(2, xq_T)

            def maxima_move(b, g):
                gi, hg, q = NG * b + g, g % HG, g // HG
                act.wait_ge(nm_T, gi + 1)
                act.activation(qstack[SHIFT:SHIFT + 3, 4 * hg:4 * hg + 4, q * 128:(q + 1) * 128],
                               nm_psum[SHIFT:SHIFT + 3, 0:512].rearrange("i (j q) -> i j q", j=4),
                               ACT.Copy).then_inc(nm_moved, 1)

            def tile_exp(b, g, t):
                n = KT * g + t
                rows = 128 if t < KFULL else KTAIL
                act.wait_ge(st_mm, NG * KT * b + n + 1)
                wait(act, xpv_mm, NG * KT * b + n - 3)
                act.activation(pT[0:rows, n % 4, :], pair[2][0:rows, (n % 2) * 512:(n % 2) * 512 + 512],
                               ACT.Exp).then_inc(expt_made, 1)

            def finish_tile(b, t, piece):
                u = 2 * b + t
                if piece == 0:
                    act.wait_ge(xpv_mm, KT * HG * (u + 1))
                    wait(act, xo_T, u)
                    act.activation(xoT, pair[3][:, 0:512], ACT.Copy).then_inc(xoT_made, 1)
                else:
                    act.wait_ge(c_T, u + 1)
                    wait(act, xproj_mm, u)
                    act.activation(cT, pair[3][:, 512:640], ACT.Copy).then_inc(cT_made, 1)

            act.wait_ge(stacks_set, 4)
            maxima_move(0, 0)

            def batch(b):
                last_batch = isinstance(b, int) and b + 1 == B
                for g in range(NG):
                    finish = g % HG == 0 and not (isinstance(b, int) and b == 0 and g == 0)
                    unit = (b, 0) if g else (b - 1, 1)
                    for t in range(KT):
                        tile_exp(b, g, t)
                        if finish and t in (0, 5):
                            finish_tile(*unit, (0, 5).index(t))
                        if t == 10 and (not last_batch or g + 1 < NG):
                            maxima_move(*((b, g + 1) if g + 1 < NG else (b + 1, 0)))

            repeat(act, B, batch)
            for piece in range(2):
                finish_tile(B - 1, 1, piece)

            std_of(3)
            xn_move(3, xnT[:, :])
            act.wait_ge(gdiff_made, 1)
            act.activation(gw[:, :, 1], gw[:, :, 0], ACT.Exp).then_inc(gexp_made, 1)

            def up_bias(m, f, e):
                wait(act, z_made, 2 * m + f - 1)
                act.wait_ge(up_mm, 2 * m + f + 1)
                bias = bias_T[:, bass.ds(2 * e + f, 1)]
                settle(act, act_tally, m)
                act.activation(x1s[:, f, :], pair[f][:, 0:512], ACT.Identity,
                               bias=bias).then_inc(x1s_made, 1)

            def gate_silu(m, half, e):
                wait(act, ogl_made, 2 * m + half - 1)
                act.wait_ge(gl_mm, 2 * m + half + 1)
                bias = bias_T[:, bass.ds(32 + 2 * e + half, 1)]
                settle(act, act_tally, m)
                act.activation(silu[:, half, :], pair[2][:, 0:512], ACT.Silu,
                               bias=bias).then_inc(silu_made, 1)

            act.wait_ge(mparts_made, 2 * B)
            up_bias(0, 0, 0)
            up_bias(0, 1, 0)
            act.wait_ge(comb_T, 1)
            act.activation(combT[:, :, :].rearrange("e t p -> e (t p)"), pair[2][0:NE, :], ACT.Copy).then_inc(combT_made, 1)

            def two_experts(r):
                more = not isinstance(r, int) or r + 1 < NE // 2
                for u in range(2):
                    for c in range(2):
                        m, e = 4 * r + 2 * u + c, 2 * r + u
                        for half in range(2):
                            gate_silu(m, half, e)
                            if (u, c) != (1, 1) or more:
                                up_bias(m + 1, half, e + c)

            repeat(act, NE // 2, two_experts)

        @block.vector
        def _(dve):
            chain = Chain(dve, dve_step)

            def layer_norm(n, src):
                for t in range(NT):
                    last = dve.bn_stats(stats[:, t, :], src[:, t, :])
                chain.step(last)
                for t in range(NT):
                    last = dve.bn_aggr(meanvar[:, t, :], stats[:, t, :])
                chain.step(last)
                dve.tensor_scalar(var_eps[:, :], meanvar[:, :, 1], LN_EPS, None, ALU.add).then_inc(var_made, 1)
                dve.wait_ge(std_made, n)
                chain.step(dve.reciprocal(rstd[:, :], std[:, :]))
                for t in range(NT):
                    last = dve.tensor_scalar(xn[:, t, :], src[:, t, :], meanvar[:, t, 0:1], rstd[:, t:t + 1],
                                             ALU.subtract, ALU.mult)
                last.then_inc(xn_made, 1)

            def truncate(out_, floor16):
                return dve.scalar_tensor_tensor(out_, floor16, 0.0, floor16, ALU.is_lt, ALU.add)

            dve.wait_ge(x_loaded, 16)
            layer_norm(1, x_in)
            dve.wait_ge(small_loaded, 16 * 10)
            chain.step(dve.tensor_scalar(bproj_fx[:, :], bproj_bc[:, :], FXP, None, ALU.mult))

            def make_qkv(hp, c):
                dve.wait_ge(qkv_rounded, 3 * hp + c + 1)
                if c < 2:
                    wait(dve, dots_mm, B * hp)
                else:
                    wait(dve, pv_mm, B * hp)
                home = (qf, kf, vf)[c]
                src = qkv16[:, c, :] if c < 2 else qkv16[:, c, :].rearrange("p (t e) -> p t e", t=NT)
                truncate(home, src).then_inc(qkv_made, 1)

            def make_dots(hp, b):
                s = B * hp + b
                dve.wait_ge(dots_rounded, s + 1)
                wait(dve, exp_made, s - 1)
                truncate(dotf[:, b % 2, :], dot16[:, b % 2, :]).then_inc(dots_made, 1)

            def make_attn(hp, b):
                s = B * hp + b
                dve.wait_ge(exp_made, s + 1)
                chain.step(dve.tensor_scalar(esum4k[:, :], esum[:, b % 2, :], 1.0 / (FXP * NUDGE), None, ALU.mult))
                chain.step(dve.reciprocal(rnorm[:, :], esum4k[:, :]))
                for k in range(4):
                    last = dve.tensor_scalar(attn_h[:, b % 2, k * 256:(k + 1) * 256], expd[:, b % 2, k * 256:(k + 1) * 256],
                                             rnorm[:, k:k + 1], -0.5, ALU.mult, ALU.add)
                chain.step(last)
                dve.tensor_scalar(attn[:, b % 2, :], attn_h[:, b % 2, :], MAGIC, MAGIC, ALU.add,
                                  ALU.subtract).then_inc(attn_made, 1)

            def make_o(hp, b):
                s = B * hp + b
                wait(dve, o_made, s)
                dve.wait_ge(pv_mm, s + 1)
                dve.tensor_scalar(o16[:, :], pair[3][:, 512:768], NUDGE / FXP, -0.5, ALU.mult, ALU.add).then_inc(o_rounded, 1)
                dve.wait_ge(o_rounded, s + 1)
                home = oT[:, hp, b * S:(b + 1) * S] if isinstance(hp, int) else \
                    region_g[:, bass.ds(hp * T + b * S, S)]
                truncate(home, o16[:, :]).then_inc(o_made, 1)

            for c in range(3):
                make_qkv(0, c)
            start, steps = chain.base + chain.n, 3 * B

            def head_pair(hp):
                chain.repetition(start, hp, steps)
                more = not isinstance(hp, int) or hp + 1 < HP
                make_dots(hp, 0)
                for b in range(B):
                    if b + 1 < B:
                        make_dots(hp, b + 1)
                    make_attn(hp, b)
                    if b >= 1:
                        make_o(hp, b - 1)
                if more:
                    make_qkv(hp + 1, 0)
                    make_qkv(hp + 1, 1)
                make_o(hp, B - 1)
                if more:
                    make_qkv(hp + 1, 2)

            repeat(dve, HP, head_pair)
            chain.after(start, HP, steps)

            dve.wait_ge(proj_mm, 1)
            flat = xn[:, :, :].rearrange("p t d -> p (t d)")
            chain.step(dve.tensor_tensor(xn[:, :, :], pair[0][:, :].rearrange("p (t d) -> p t d", t=NT),
                                         bproj_fx[:, :].unsqueeze(1).broadcast_to([128, NT, D]), ALU.add))
            chain.step(dve.tensor_scalar(qkv16[:, 0, :], flat, NUDGE, -0.5, ALU.mult, ALU.add))
            chain.step(truncate(flat, qkv16[:, 0, :]))
            dve.scalar_tensor_tensor(x1[:, :, :], xn[:, :, :], 1.0 / FXP, x_in[:, :, :], ALU.mult,
                                     ALU.add).then_inc(x1_made, 1)
            dve.wait_ge(x1_made, 1)
            layer_norm(2, x1)
            dve.wait_ge(xnT_made, 2)
            for i in range(3):
                if i < 2:
                    chain.step(dve.tensor_copy(qparts[:, i, :], xq_T))
                    chain.step(dve.tensor_tensor(xq_T, xq_T, qparts[:, i, :], ALU.subtract))
                else:
                    dve.tensor_copy(qparts[:, i, :], xq_T).then_inc(qparts_made, 1)

            def row_maximum(b, g, j):
                gi, t = NG * b + g, g // HG
                if j == 0 and g % HG == 0:
                    dve.wait_ge(mask_loaded[t], 16 * (b + 1))
                for c, (k0, size) in enumerate(CHUNKS):
                    if c == 0:
                        wait(dve, half_made, 4 * gi + j)
                        wait(dve, nparts_made, gi - 1)
                        first = 3.0e38
                    else:
                        wait(dve, masked_made, 4 * gi + j)
                        dve.wait_ge(half_made, 4 * gi + j + 1)
                        first = nmax[:, g % 2, j, 0:1]
                    dve.wait_ge(score_mm, 8 * gi + 2 * j + c + 1)
                    settle(dve, dve_tally, b)
                    dve.tensor_tensor_reduce(out=unused[c][:, 0:size], in0=pair[c][:, 0:size],
                                             in1=mask_sb[:, t, k0:k0 + size], scale=-1.0, scalar=first,
                                             op0=ALU.add, op1=ALU.min,
                                             accum_out=nmax[:, g % 2, j, c:c + 1]).then_inc((half_made, masked_made)[c], 1)

            def split_maxima(b, g):
                gi = NG * b + g
                dve.wait_ge(masked_made, 4 * gi + 4)
                wait(dve, nm_T, gi - 1)
                src = nmax[:, g % 2, :, 1]
                for i in range(3):
                    if i < 2:
                        chain.step(dve.tensor_copy(nparts[:, g % 2, :, i], src))
                        chain.step(dve.tensor_tensor(nrest[:, :], src, nparts[:, g % 2, :, i], ALU.subtract))
                        src = nrest[:, :]
                    else:
                        dve.tensor_copy(nparts[:, g % 2, :, i], src).then_inc(nparts_made, 1)

            def mask_largest(b, t):
                u = 2 * b + t
                dve.wait_ge(mask_loaded[t], 16 * (b + 1))
                wait(dve, flag_made, u - 1)
                chain.step(dve.tensor_reduce(mask_hi[:, 0:1], mask_sb[:, t, :], AX.X, ALU.max))
                chain.step(dve.tensor_reduce(mask_hi[:, 1:2], mask_sb[:, t, :], AX.X, ALU.min))
                dve.scalar_tensor_tensor(mask_any[:, t:t + 1], mask_hi[:, 1:2], -1.0, mask_hi[:, 0:1], ALU.mult,
                                         ALU.max).then_inc(any_made, 1)

            def finish_tile(b, t, piece):
                u = 2 * b + t
                if piece == 0:
                    dve.wait_ge(xo_T, u + 1)
                    heads = pair[3][:, 512:1024].rearrange("p (h c) -> p h c", h=H)
                    chain.step(dve.reciprocal(rsum_x[:, :], heads[:, :, XD]))
                    wait(dve, c_T, u)
                    dve.tensor_tensor(cnat.rearrange("p (h c) -> p h c", h=H), heads[:, :, 0:XD],
                                      rsum_x[:, :].unsqueeze(2).broadcast_to([128, H, XD]), ALU.mult).then_inc(cnat_made, 1)
                else:
                    dve.wait_ge(xproj_mm, u + 1)
                    wait(dve, x2_made, u)
                    dve.tensor_tensor(xo[:, :], pair[3][:, 640:768], wob_bc[:, :], ALU.add).then_inc(xbias_made, 1)
                    dve.wait_ge(xbias_made, u + 1)
                    tile = slice(u, u + 1) if isinstance(u, int) else bass.ds(u, 1)
                    dve.scalar_tensor_tensor(acc[:, tile, :], xo[:, :].unsqueeze(1), 0.0, x1[:, tile, :], ALU.max,
                                             ALU.add).then_inc(x2_made, 1)

            def head_of(b, g, j, ahead):
                n = 4 * g + j + ahead
                return (b, n // 4, n % 4) if n < 4 * NG else (b + 1, n // 4 - NG, n % 4)

            mask_largest(0, 0)
            for n in range(AHEAD):
                row_maximum(*head_of(0, 0, 0, n))
                if n == 3:
                    split_maxima(0, 0)
            start, steps = chain.base + chain.n, NG * 4 + 2 + 2 * 2

            def batch(b):
                chain.repetition(start, b, steps)
                last_batch = isinstance(b, int) and b + 1 == B
                for g in range(NG):
                    finish = g % HG == 0 and not (isinstance(b, int) and b == 0 and g == 0)
                    unit = (b, 0) if g else (b - 1, 1)
                    for j in range(4):
                        if not last_batch or 4 * g + j + AHEAD < 4 * NG:
                            row_maximum(*head_of(b, g, j, AHEAD))
                        if j == 1 and (not last_batch or g + 1 < NG):
                            split_maxima(*((b, g + 1) if g + 1 < NG else (b + 1, 0)))
                        if j == 2 and g == 1:
                            mask_largest(b, 1)
                        if j == 2 and g == 5 and not last_batch:
                            mask_largest(b + 1, 0)
                        if finish and j == 0:
                            finish_tile(*unit, 0)
                        if finish and j == 2:
                            finish_tile(*unit, 1)
                if isinstance(b, int) and b == 0:
                    chain.n += 1
                    dve.sem_inc(dve_step, 1)
                if last_batch:
                    chain.n += 4 + 2
                    dve.sem_inc(dve_step, 4 + 2)

            repeat(dve, B, batch)
            chain.after(start, B, steps)
            finish_tile(B - 1, 1, 0)
            finish_tile(B - 1, 1, 1)

            dve.wait_ge(x2_made, 2 * B)
            layer_norm(3, acc)
            dve.wait_ge(gate_mm, 1)
            chain.step(dve.tensor_tensor(gate[:, :, :], pair[3][:, 0:NT * NE].rearrange("p (t e) -> p t e", t=NT),
                                         bgate_bc[:, :].unsqueeze(1).broadcast_to([128, NT, NE]), ALU.add))
            for t in range(NT):
                last = dve.max(gtop[:, t, :], gate[:, t, :])
            chain.step(last)
            dve.tensor_tensor(gw[:, :, 0], gtop[:, :, 1], gtop[:, :, 0], ALU.subtract).then_inc(gdiff_made, 1)
            for t in range(NT):
                last = dve.max_index(gidx[:, t, :], gtop[:, t, :], gate[:, t, :])
            chain.step(last)
            chain.step(dve.tensor_copy(gidf[:, :, :], gidx[:, :, :]))
            dve.wait_ge(gexp_made, 1)
            chain.step(dve.tensor_scalar(gw[:, :, 2], gw[:, :, 1], 1.0, None, ALU.add))
            chain.step(dve.reciprocal(gw[:, :, 3], gw[:, :, 2]))
            chain.step(dve.tensor_tensor(gw[:, :, 2], gw[:, :, 1], gw[:, :, 3], ALU.mult))
            dve.wait_ge(iota_made, 1)
            every = [128, NT, NE]
            for k in range(2):
                last = dve.tensor_tensor(pick[:, k, :, :], iota_e[:, :].unsqueeze(1).broadcast_to(every),
                                         gidf[:, :, k:k + 1].broadcast_to(every), ALU.is_equal)
            chain.step(last)
            for k in range(2):
                last = dve.tensor_tensor(pick[:, k, :, :], pick[:, k, :, :],
                                         gw[:, :, 3 - k:4 - k].broadcast_to(every), ALU.mult)
            chain.step(last)
            dve.tensor_tensor(comb[:, :, :].rearrange("p e t -> p t e"), pick[:, 0, :, :], pick[:, 1, :, :],
                              ALU.add).then_inc(comb_made, 1)

            def zed_of(m, f, e, c):
                dve.wait_ge(x1s_made, 2 * m + f + 1)
                wait(dve, gl_mm, 2 * m - 2)
                dve.scalar_tensor_tensor(zed[:, c, f, :], pair[f][:, 512:1024], bias_T[:, bass.ds(16 + 2 * e + f, 1)],
                                         x1s[:, f, :], ALU.add, ALU.mult).then_inc(z_made, 1)

            def ogl_of(m, half, e, c):
                dve.wait_ge(silu_made, 2 * m + half + 1)
                wait(dve, y_mm, m - 1)
                dve.scalar_tensor_tensor(ogl[:, c, half, :], pair[2][:, 512:1024], bias_T[:, bass.ds(48 + 2 * e + half, 1)],
                                         silu[:, half, :], ALU.add, ALU.mult).then_inc(ogl_made, 1)

            def add_expert(m, e, c):
                dve.wait_ge(y_mm, m + 1)
                wait(dve, y_added, m - 1)
                weight = comb[:, :, :].rearrange("p e t -> p (e t)")
                for t in range(4):
                    last = dve.scalar_tensor_tensor(acc[:, 4 * c + t, :], pair[3][:, c * 512 + t * 128:c * 512 + (t + 1) * 128],
                                                    weight[:, bass.ds(e * NT + 4 * c + t, 1)], acc[:, 4 * c + t, :],
                                                    ALU.mult, ALU.add)
                last.then_inc(y_added, 1)

            zed_of(0, 0, 0, 0)
            zed_of(0, 1, 0, 0)
            dve.wait_ge(b3_mm, 1)
            dve.tensor_tensor(acc[:, :, :], acc[:, :, :], pair[3][:, :].rearrange("p (t d) -> p t d", t=NT),
                              ALU.add).then_inc(acc_made, 1)
            dve.wait_ge(acc_made, 1)

            def two_experts(r):
                more = not isinstance(r, int) or r + 1 < NE // 2
                for u in range(2):
                    for c in range(2):
                        m, e = 4 * r + 2 * u + c, 2 * r + u
                        for half in range(2):
                            ogl_of(m, half, e, c)
                            if (u, c) != (1, 1) or more:
                                zed_of(m + 1, half, e + c, 1 - c)
                        add_expert(m, e, c)

            repeat(dve, NE // 2, two_experts)


_INS = ['x', 'ctx_1024', 'mask_Bx1xSxS2_ff0', 'L0_attn_w_qkv', 'L0_attn_w_proj', 'L0_attn_b_proj',
        'L0_xattn_wo_w', 'L0_xattn_wo_b', 'L0_ffn_Wgate', 'L0_ffn_bgate', 'L0_ffn_W1', 'L0_ffn_b1',
        'L0_ffn_W2', 'L0_ffn_b2', 'L0_ffn_Wg', 'L0_ffn_bg', 'L0_ffn_Wl', 'L0_ffn_bl', 'L0_ffn_W3', 'L0_ffn_b3']


def kernel(**inputs):
    import numpy as _np
    import concourse.bacc as _bacc
    from concourse import mybir as _mybir
    from concourse.bass_utils import run_bass_kernel_spmd as _run

    nc = _bacc.Bacc("TRN2", target_bir_lowering=False, num_devices=1)
    arrays, args = {}, []
    for name in _INS:
        a = _np.ascontiguousarray(inputs[name])
        arrays[f"in_{name}"] = a
        args.append(nc.dram_tensor(f"in_{name}", a.shape, _mybir.dt.from_np(a.dtype), kind="ExternalInput").ap())
    out = nc.dram_tensor("out", (4, 256, 128), _mybir.dt.float32, kind="ExternalOutput").ap()
    decoder_layer(nc, *args, out)
    r = _run(nc, [arrays], core_ids=[0])
    return r.results[0]["out"]
```

```python
import concourse.bass as bass
from concourse import mybir
from contextlib import ExitStack

F32 = mybir.dt.float32
BF16 = mybir.dt.bfloat16
I16 = mybir.dt.int16
U32 = mybir.dt.uint32
ALU = mybir.AluOpType
ACT = mybir.ActivationFunctionType
AX = mybir.AxisListType
RMAX = bass.bass_isa.ReduceOp.max

B, S, D = 4, 256, 128
T = B * S
NT = T // 128
S2 = 1601
KT = (S2 + 127) // 128
KFULL = S2 // 128
KTAIL = S2 - KFULL * 128
H, DH = 16, 64
HP = H // 2
XD = D // H
HG = H // 4
NE, FF = 8, 256
NG = 2 * HG

FXP = 4096.0
NUDGE = 1.0 + 2.0 ** -22
LN_EPS = 1e-5
LOWEST = -3.0e38
MAGIC = 1.5 * 2.0 ** 23

OUT_TILES = ((0, S // 128), (S // 128, NT))

FFN_TILES = ((0, NT - S // 128), (NT - S // 128, NT))

CHUNKS = ((0, 1024), (1024, S2 - 1024))
AHEAD = 8
AHEAD_AT = ((0, 4, 7, 10), (2, 6, 9, 12))
MASK_AT = ((4, 0), (4, 1), (4, 2), (4, 3), (6, 2), (6, 3), (7, 0), (7, 1))
SROWS = 96
SHIFT = 96
ONE_BF16_TWICE = 1.0 + 0x3F80 / 2.0 ** 23


class Chain:

    def __init__(self, eng, sem):
        self.eng, self.sem, self.base, self.n = eng, sem, 0, 0

    def step(self, ins):
        self.n += 1
        ins.then_inc(self.sem, 1)
        self.eng.wait_ge(self.sem, self.base + self.n)

    def later(self, ins):
        self.n += 1
        ins.then_inc(self.sem, 1)

    def join(self):
        self.eng.wait_ge(self.sem, self.base + self.n)

    def repetition(self, start, i, steps):
        self.base, self.n = start + i * steps, 0

    def after(self, start, repetitions, steps):
        assert self.n == steps, (self.n, steps)
        self.base, self.n = start + repetitions * steps, 0


def wait(eng, semaphore, value):
    if not isinstance(value, int) or value > 0:
        eng.wait_ge(semaphore, value)


def settle(eng, tally, i):
    if not isinstance(i, int):
        eng.sem_inc(tally, 1)


def batch_of(hp, b, steps):
    n = b + steps
    return (hp, n) if 0 <= n < B else (hp + 1, n - B) if n >= B else (hp - 1, n + B)


def maxima_at(finish):
    return 9 if finish else 8


def repeat(eng, count, body):
    body(0)
    with eng.Fori(1, count - 1) as i:
        body(i)
    body(count - 1)


def decoder_layer(nc, x, ctx_in, mask, w_qkv, w_proj, b_proj, wo_w, wo_b, Wgate, bgate,
                  W1, b1, W2, b2, Wg, bg, Wl, bl, W3, b3, out):
    stack = ExitStack()
    with stack:
        def sb(name, shape, dt=F32):
            return stack.enter_context(nc.sbuf_tensor(name, shape, dt))

        def sem(name):
            return stack.enter_context(nc.semaphore(name))

        ident = sb("ident", [128, 128])
        x_in = sb("x_in", [128, NT, D])
        x1 = sb("x1", [128, NT, D])
        acc = x_in
        xn = sb("xn", [128, NT, D])
        xnT = sb("xnT", [128, T])
        stats = sb("stats", [128, NT, 6])
        meanvar = sb("meanvar", [128, NT, 2])
        var_eps = sb("var_eps", [128, NT])
        std = sb("std", [128, NT])
        rstd = sb("rstd", [128, NT])
        wnat = sb("wnat", [128, 3, D])
        wT = sb("wT", [128, 3 * 128])
        woT = sb("woT", [128, D])
        bproj_bc = sb("bproj_bc", [128, D])
        bproj_fx = sb("bproj_fx", [128, D])
        wob_bc = sb("wob_bc", [128, D])
        bgate_bc = sb("bgate_bc", [128, NE])
        wgate = sb("wgate", [128, NE])
        bias_nat = sb("bias_nat", [64, 128])
        bias_T = sb("bias_T", [128, 64])
        b3_sb = sb("b3_sb", [NE, D])
        esum = sb("esum", [128, 2, 4])
        esum4k = sb("esum4k", [128, 4])
        rnorm = sb("rnorm", [128, 4])
        o16 = sb("o16", [128, S], I16)
        nmax = sb("nmax", [128, 2, 4, 2])
        nparts = sb("nparts", [128, 2, 4, 3], BF16)
        nrest = sb("nrest", [128, 4])
        mask_hi = sb("mask_hi", [128, 8])
        mask_any = sb("mask_any", [128, 1])
        mask_flag = sb("mask_flag", [128, 1])
        warm = sb("warm", [128, 1])
        identb = sb("identb", [128, 128], BF16)
        rsum_x = sb("rsum_x", [128, H])
        xo = sb("xo", [128, D])
        gate = sb("gate", [128, NT, NE])
        gtop = sb("gtop", [128, NT, 8])
        gidx = sb("gidx", [128, NT, 8], U32)
        gidf = sb("gidf", [128, NT, 8])
        gw = sb("gw", [128, NT, 4])
        iota_e = sb("iota_e", [128, NE])
        pick = sb("pick", [128, 2, NT, NE])
        comb = sb("comb", [128, NE, NT])
        combT = sb("combT", [NE, NT, 128])
        qstack = sb("qstack", [128, H, S], BF16)
        mask_sb = sb("mask_sb", [128, 2, S2])
        v_nat = mask_sb[:, :, :].rearrange("p t k -> p (t k)")[:, 0:KT * D].rearrange("p (t d) -> p t d", t=KT)
        v_next = sb("v_next", [128, KT, D])
        VW = XD + 1
        v_aug = sb("v_aug", [128, KT, H * VW + 32 - VW])
        pT = sb("pT", [128, 4, 512])
        wpT = pT[:, 0:2, :].rearrange("p u k -> p (u k)").rearrange("p (h d) -> p h d", h=HP)

        region_k = sb("region_k", [128, 8 * S2])
        kstack = region_k[:, :].bitcast(BF16).rearrange("p (h k) -> p h k", h=H)
        ctxT = region_k[:, 0:4 * S2].rearrange("p (u k) -> p u k", u=4)
        kparts = region_k[:, 4 * S2:7 * S2].bitcast(BF16).rearrange("p (u i k) -> p u i k", u=2, i=3)

        region_p = sb("region_p", [128, 8 * S2])
        at = 0

        def cut(region, size):
            nonlocal at
            at += size
            return region[:, at - size:at]

        qf = cut(region_p, T)
        kf = cut(region_p, T)
        vf = cut(region_p, T).rearrange("p (t e) -> p t e", t=NT)
        qkv16 = cut(region_p, 3 * T // 2).bitcast(I16).rearrange("p (c t) -> p c t", c=3)
        dot16 = cut(region_p, T).bitcast(I16).rearrange("p (u k) -> p u k", u=2)
        dotf = cut(region_p, T).bitcast(I16).rearrange("p (u k) -> p u k", u=2)
        expd = cut(region_p, 2 * T).rearrange("p (u k) -> p u k", u=2)
        attn_h = cut(region_p, 2 * T).rearrange("p (u k) -> p u k", u=2)
        attn = expd
        attnT = cut(region_p, T)
        assert at <= 8 * S2
        at = 0
        mparts = cut(region_p, 3 * S2).bitcast(BF16).rearrange("p (u i k) -> p u i k", u=2, i=3)
        mrest = cut(region_p, S2)
        unused = [cut(region_p, 1024), cut(region_p, 1024)]
        xoT = cut(region_p, HG * 128)
        cnat = cut(region_p, D)
        cT = cut(region_p, 128)
        assert at <= 8 * S2
        at = 0
        x1s = cut(region_p, 2 * 512).rearrange("p (f t) -> p f t", f=2)
        zed = cut(region_p, 4 * 512).rearrange("p (u f t) -> p u f t", u=2, f=2)
        silu = cut(region_p, 2 * 512).rearrange("p (f t) -> p f t", f=2)
        ogl = cut(region_p, 4 * 512).rearrange("p (u f t) -> p u f t", u=2, f=2)

        region_g = sb("region_g", [128, HP * T])
        oT = region_g[:, :].rearrange("p (h t) -> p h t", h=HP)
        at = 0
        w1_sb = cut(region_g, 2 * FF).rearrange("p (u f) -> p u f", u=2)
        w2_sb = cut(region_g, 2 * FF).rearrange("p (u f) -> p u f", u=2)
        wg_sb = cut(region_g, 4 * FF).rearrange("p (u k f) -> p u k f", u=2, k=2)
        wl_sb = cut(region_g, 4 * FF).rearrange("p (u k f) -> p u k f", u=2, k=2)
        w3_sb = cut(region_g, 4 * D).rearrange("p (u k f) -> p u k f", u=2, k=2)
        xq_T = cut(region_g, T)
        qparts = cut(region_g, 3 * T // 2).bitcast(BF16).rearrange("p (j t) -> p j t", j=3)

        pair = [stack.enter_context(nc.psum_tensor(f"pair{i}", [128, 1024], F32)) for i in range(4)]
        nm_psum = pair[3][:, 512:768].bitcast(BF16)

        def qkv_home(hp, c):
            return pair[(2, 0, 1)[c]] if isinstance(hp, int) and hp == 0 else pair[2]

        kscr = nc.dram_tensor("kscr", (B, H * XD, 3 * S2), BF16, kind="Internal").ap()
        qscr = nc.dram_tensor("qscr", (3, H * XD, 3, T), BF16, kind="Internal").ap()

        x_loaded = sem("x_loaded")
        small_loaded = sem("small_loaded")
        wproj_loaded = sem("wproj_loaded")
        ctx_loaded = [sem("ctx_loaded_even"), sem("ctx_loaded_odd")]
        wnat_loaded = sem("wnat_loaded")
        mask_loaded = [sem("mask_loaded_0"), sem("mask_loaded_1")]
        kq_loaded = [sem(f"kq_loaded_{g}") for g in range(HG)]
        kscr_written = [sem("kscr_written_even"), sem("kscr_written_odd")]
        qscr_written = sem("qscr_written")
        v_loaded = sem("v_loaded")
        wexp_loaded = [sem("wexp_loaded_0"), sem("wexp_loaded_1")]
        out_written = sem("out_written")

        act_tally = sem("act_tally")
        pe_tally = sem("pe_tally")
        dve_tally = sem("dve_tally")
        pool_step = sem("pool_step")
        dve_step = sem("dve_step")
        ident_made = sem("ident_made")
        iota_made = sem("iota_made")
        wproj_T = sem("wproj_T")
        wpT_made = sem("wpT_made")
        small_T = sem("small_T")
        smallT_made = sem("smallT_made")
        ctx_T = sem("ctx_T")
        ctxT_made = sem("ctxT_made")
        kparts_made = sem("kparts_made")
        var_made = sem("var_made")
        std_made = sem("std_made")
        xn_made = sem("xn_made")
        xn_T = sem("xn_T")
        xnT_made = sem("xnT_made")

        w_T = sem("w_T")
        wT_made = sem("wT_made")
        qkv_mm = sem("qkv_mm")
        qkv_rounded = sem("qkv_rounded")
        qkv_made = sem("qkv_made")
        dots_mm = sem("dots_mm")
        dots_rounded = sem("dots_rounded")
        dots_made = sem("dots_made")
        exp_made = sem("exp_made")
        attn_made = sem("attn_made")
        attn_T = sem("attn_T")
        attnT_made = sem("attnT_made")
        pv_mm = sem("pv_mm")
        o_rounded = sem("o_rounded")
        o_made = sem("o_made")
        proj_mm = sem("proj_mm")
        x1_made = sem("x1_made")
        qparts_made = sem("qparts_made")
        part_made = sem("part_made")
        rest_made = sem("rest_made")

        stacks_set = sem("stacks_set")
        score_mm = sem("score_mm")
        half_made = sem("half_made")
        masked_made = sem("masked_made")
        nparts_made = sem("nparts_made")
        nm_T = sem("nm_T")
        nm_moved = sem("nm_moved")
        any_made = sem("any_made")
        flag_made = sem("flag_made")
        mparts_made = sem("mparts_made")
        v0_made = sem("v0_made")
        st_mm = sem("st_mm")
        expt_made = sem("expt_made")
        xpv_mm = sem("xpv_mm")
        v_moved = sem("v_moved")
        xoT_made = sem("xoT_made")
        xo_T = sem("xo_T")
        cnat_made = sem("cnat_made")
        c_T = sem("c_T")
        cT_made = sem("cT_made")
        xproj_mm = sem("xproj_mm")
        xbias_made = sem("xbias_made")
        x2_made = sem("x2_made")

        gate_mm = sem("gate_mm")
        gdiff_made = sem("gdiff_made")
        gexp_made = sem("gexp_made")
        comb_made = sem("comb_made")
        comb_T = sem("comb_T")
        combT_made = sem("combT_made")
        b3_mm = sem("b3_mm")
        acc_made = sem("acc_made")
        up_mm = sem("up_mm")
        x1s_made = sem("x1s_made")
        z_made = sem("z_made")
        gl_mm = sem("gl_mm")
        silu_made = sem("silu_made")
        ogl_made = sem("ogl_made")
        y_mm = sem("y_mm")
        y_added = sem("y_added")

        block = stack.enter_context(nc.Block())

        x_tiles = x.rearrange("b (t p) d -> p (b t) d", p=128)
        out_tiles = out.rearrange("b (t p) d -> p (b t) d", p=128)
        w_rows = w_qkv.rearrange("(c e) d -> e c d", c=3)
        mask_tiles = mask.rearrange("b a (t p) k -> (b a) t p k", p=128)
        CTX_ORDER = (2, 3, 0, 1)
        ctx_home = (v_nat, v_next, v_nat, v_next)

        def ctx_load(eng, b, home, signal):
            eng.dma_start(home[:, 0:KFULL, :],
                          ctx_in[b, 0:KFULL * 128, :].rearrange("(t p) d -> p t d", p=128)).then_inc(signal, 16)
            eng.dma_start(home[0:KTAIL, KFULL, :], ctx_in[b, KFULL * 128:S2, :]).then_inc(signal, 16)

        def expert_load(sp, e, u):
            sp.dma_start(w1_sb[:, u, :], W1[e]).then_inc(wexp_loaded[u], 16)
            sp.dma_start(w2_sb[:, u, :], W2[e]).then_inc(wexp_loaded[u], 16)
            sp.dma_start(wg_sb[:, u, :, :], Wg[e].rearrange("(k p) f -> p k f", p=128)).then_inc(wexp_loaded[u], 16)
            sp.dma_start(wl_sb[:, u, :, :], Wl[e].rearrange("(k p) f -> p k f", p=128)).then_inc(wexp_loaded[u], 16)
            sp.dma_start(w3_sb[:, u, :, :], W3[e].rearrange("(k p) f -> p k f", p=128)).then_inc(wexp_loaded[u], 16)

        @block.sync
        def _(sp):
            sp.dma_start(x_in[:, :, :], x_tiles).then_inc(x_loaded, 16)
            sp.dma_start(wnat[:, :, :], w_rows[0:128, :, :]).then_inc(wnat_loaded, 16)
            sp.dma_start(x1[:, :, :].rearrange("p t d -> p (t d)"), w_proj).then_inc(wproj_loaded, 16)
            for k in range(2):
                ctx_load(sp, CTX_ORDER[k], ctx_home[k], ctx_loaded[k % 2])
            sp.dma_start(xo[:, :], wo_w).then_inc(small_loaded, 16)
            for n, v in enumerate((b1, b2, bg, bl)):
                sp.dma_start(bias_nat[16 * n:16 * n + 16, :], v.rearrange("e (h f) -> (e h) f", h=2)).then_inc(small_loaded, 16)
            sp.dma_start(bproj_bc[:, :], b_proj.partition_broadcast(128)).then_inc(small_loaded, 16)
            sp.dma_start(wob_bc[:, :], wo_b.partition_broadcast(128)).then_inc(small_loaded, 16)
            sp.dma_start(bgate_bc[:, :], bgate.partition_broadcast(128)).then_inc(small_loaded, 16)
            sp.dma_start(wgate[:, :], Wgate).then_inc(small_loaded, 16)
            sp.dma_start(b3_sb[:, :], b3).then_inc(small_loaded, 16)
            def weights_load(hp):
                sp.wait_ge(w_T, hp)
                sp.dma_start(wnat[:, :, :], w_rows[bass.ds(hp * 128, 128), :, :]).then_inc(wnat_loaded, 16)

            for k in range(2, 4):
                sp.wait_ge(ctx_T, 2 * (k - 1))
                ctx_load(sp, CTX_ORDER[k], ctx_home[k], ctx_loaded[k % 2])
                if k == 2:
                    weights_load(1)
            with sp.Fori(2, HP) as hp:
                weights_load(hp)

            def keys_load(b, g):
                ksrc = kscr[b].rearrange("(h d) (i k) -> h (d i) k", h=H, i=3)[4 * g:4 * g + 4]
                for j in range(3):
                    sp.dma_start(kstack[24 * j:24 * j + 24, 4 * g:4 * g + 4, :],
                                 ksrc.rearrange("h r k -> r h k")).then_inc(kq_loaded[g], 16)

            def queries_load(b, g):
                for j in range(3):
                    qsrc = qscr[j].rearrange("(h d) i t -> h (d i) t", h=H)[4 * g:4 * g + 4, :, bass.ds(b * S, S)]
                    sp.dma_start(qstack[24 * j:24 * j + 24, 4 * g:4 * g + 4, :],
                                 qsrc.rearrange("h r t -> r h t")).then_inc(kq_loaded[g], 16)

            def queries_store(c):
                sp.wait_ge(qparts_made, c + 1)
                tokens = slice(128 * OUT_TILES[c][0], 128 * OUT_TILES[c][1])
                size = tokens.stop - tokens.start
                for j in range(3):
                    sp.dma_start(qscr[j, :, :, tokens], qparts[:, j:j + 1, tokens].broadcast_to([128, 3, size])
                                 ).then_inc(qscr_written, 16)

            sp.wait_ge(v0_made, 2)
            for t in range(2):
                sp.dma_start(mask_sb[:, t, :], mask_tiles[0, t]).then_inc(mask_loaded[t], 16)
            sp.wait_ge(stacks_set, 4)
            for g in range(HG):
                keys_load(0, g)
            queries_store(0)
            sp.wait_ge(qscr_written, 16 * 3)
            for g in range(HG):
                queries_load(0, g)
            queries_store(1)
            for u in range(2):
                expert_load(sp, u, u)
            sp.wait_ge(qscr_written, 16 * 6)

            def mask_load(b, t):
                u = 2 * b + t
                sp.wait_ge(masked_made, 16 * (u - 1))
                sp.wait_ge(mparts_made, u - 1)
                sp.wait_ge(any_made, b)
                sp.dma_start(mask_sb[:, t, :], mask_tiles[b, t]).then_inc(mask_loaded[t], 16)

            with sp.Fori(1, B) as b:
                mask_load(b, 0)
                for g in range(HG):
                    sp.wait_ge(st_mm, KT * (NG * (b - 1) + HG + g + 1))
                    keys_load(b, g)
                    queries_load(b, g)
                    if g == 1:
                        mask_load(b, 1)
            with sp.Fori(1, NE // 2) as r:
                for u in range(2):
                    sp.wait_ge(y_mm, 4 * r - 2 + 2 * u)
                    expert_load(sp, 2 * r + u, u)
            sp.wait_ge(y_added, 2 * NE)
            sp.dma_start(out_tiles, acc[:, :, :]).then_inc(out_written, 16)
            sp.wait_ge(out_written, 16)

        @block.gpsimd
        def _(pool):
            chain = Chain(pool, pool_step)
            chain.step(pool.memset(ident[:, :], 0.0))
            pool.affine_select(out=ident[:, :], in_=ident[:, :], compare_op=ALU.not_equal, fill=1.0, base=0,
                               pattern=[[-1, 128]], channel_multiplier=1).then_inc(ident_made, 1)
            pool.iota(iota_e[:, :], pattern=[[1, NE]], base=0, channel_multiplier=0,
                      allow_small_or_imprecise_dtypes=True).then_inc(iota_made, 1)
            pool.wait_ge(ident_made, 1)
            pool.tensor_copy(identb[:, :], ident[:, :]).then_inc(ident_made, 1)
            pool.wait_ge(ident_made, 2)
            pool.memset(qstack[64:96, :, :].rearrange("p h t -> p (h t)").bitcast(F32), 0.0).then_inc(stacks_set, 1)
            pool.wait_ge(stacks_set, 1)
            chain.step(pool.memset(v_aug[:, :, :], 1.0))

            def split(parts, rest, src, signal):
                for i in range(3):
                    if i < 2:
                        chain.step(pool.tensor_copy(parts[:, i, :], src))
                        chain.step(pool.tensor_tensor(rest, src, parts[:, i, :], ALU.subtract))
                        src = rest
                    else:
                        pool.tensor_copy(parts[:, i, :], src).then_inc(signal, 1)

            def move_values(nat, g, signal):
                for rows, tiles in ((128, slice(0, KFULL)), (KTAIL, slice(KFULL, KT))):
                    dst = v_aug[0:rows, tiles, 4 * VW * g:4 * VW * (g + 1)].rearrange("p t (j c) -> p t j c", j=4)
                    src = nat[0:rows, tiles, 32 * g:32 * g + 32].rearrange("p t (j c) -> p t j c", j=4)
                    pool.tensor_copy(dst[:, :, :, 0:XD], src).then_inc(signal, 1)

            for k, b in enumerate(CTX_ORDER):
                pool.wait_ge(ctxT_made, 2 * k + 2)
                if k >= 2:
                    pool.wait_ge(kscr_written[k % 2], 16)
                split(kparts[:, k % 2, :, :], ctxT[:, k, :], ctxT[:, k, :], kparts_made)
                pool.wait_ge(kparts_made, k + 1)
                pool.dma_start(kscr[b], kparts[:, k % 2, :, :].rearrange("p i k -> p (i k)")).then_inc(kscr_written[k % 2], 16)
            for g in range(HG):
                move_values(v_nat, g, pool_step)
            chain.n += 2 * HG
            pool.wait_ge(pool_step, chain.base + chain.n)
            pool.sem_inc(v0_made, 2)
            for k in range(2):
                pool.wait_ge(kscr_written[k], 32)
            pool.memset(region_k[64:96, :], 0.0).then_inc(stacks_set, 1)
            pool.wait_ge(stacks_set, 2)
            pool.memset(region_k[SHIFT:SHIFT + 3, :], ONE_BF16_TWICE).then_inc(stacks_set, 1)
            pool.wait_ge(stacks_set, 3)
            pool.sem_inc(stacks_set, 1)

            def mask_split(b, t):
                u = 2 * b + t
                pool.wait_ge(mask_loaded[t], 16 * (b + 1))
                if u >= 2:
                    pool.wait_ge(st_mm, KT * HG * (u - 1))
                if u:
                    pool.wait_ge(mparts_made, u)
                chain.step(pool.tensor_scalar(mrest, mask_sb[:, t, :], LOWEST, None, ALU.max))
                split(mparts[:, t, :, :], mrest, mrest, mparts_made)

            def flag_of(b):
                pool.wait_ge(any_made, b + 1)
                pool.partition_all_reduce(mask_flag[:, :], mask_any[:, :], 128, RMAX).then_inc(flag_made, 1)

            pool.wait_ge(x1_made, 1)
            flag_of(0)
            mask_split(0, 0)
            pool.wait_ge(x1_made, 2)
            mask_split(0, 1)
            for b in range(1, B):
                mask_split(b, 0)
                if b == 1:
                    pool.wait_ge(ctx_loaded[1], 64)
                else:
                    pool.wait_ge(v_loaded, 32 * (b - 1))
                for g in range(HG):
                    if g + 1 == HG:
                        flag_of(b)
                    pool.wait_ge(xpv_mm, KT * (NG * (b - 1) + HG + g + 1))
                    move_values(v_next, g, v_moved)
                if b + 1 < B:
                    pool.wait_ge(v_moved, 8 * b)
                    ctx_load(pool, b + 1, v_next, v_loaded)
                mask_split(b, 1)

        @block.tensor
        def _(pe):
            pe.wait_ge(ident_made, 1)
            pe.wait_ge(wproj_loaded, 16)
            wproj_nat = x1[:, :, :].rearrange("p t d -> p (t d)")
            for n in range(HP):
                last = pe.transpose(pair[3][:, n * 128:(n + 1) * 128], wproj_nat[:, n * 128:(n + 1) * 128], ident[:, :])
            last.then_inc(wproj_T, 1)

            def ctx_transposes(k, pairs):
                pe.wait_ge(ctx_loaded[k % 2], 32 * (k // 2 + 1))
                for half, tiles in enumerate((range(0, 8), range(8, KT))):
                    if k:
                        pe.wait_ge(ctxT_made, 2 * k + half)
                        pe.wait_ge(qkv_rounded, 3 + min(k + 1, 3))
                    for t in tiles:
                        rows = 128 if t < KFULL else KTAIL
                        c = (t % 8) * 128
                        last = pe.transpose(pair[pairs[half]][:, c:c + rows], ctx_home[k][0:rows, t, :], ident[0:rows, 0:rows])
                    last.then_inc(ctx_T, 1)

            def xn_transposes(n, home, tiles):
                pe.wait_ge(xn_made, n)
                for i, t in enumerate(range(*tiles)):
                    last = pe.transpose(home[:, i * 128:(i + 1) * 128], xn[:, t, :], ident[:, :])
                last.then_inc(xn_T, 1)

            ctx_transposes(0, (0, 1))
            xn_transposes(1, pair[2], (0, NT))
            pe.wait_ge(wpT_made, 1)
            pe.wait_ge(small_loaded, 16 * 10)
            pe.transpose(pair[3][:, 0:128], xo[:, :], ident[:, :])
            pe.transpose(pair[3][:, 128:192], bias_nat[:, :], ident[0:64, 0:64]).then_inc(small_T, 1)

            def weights_T(hp):
                pe.wait_ge(wnat_loaded, 16 * (hp + 1))
                if isinstance(hp, int) and hp == 0:
                    pe.wait_ge(smallT_made, 2)
                for c in range(3):
                    last = pe.transpose(pair[3][:, c * 128:(c + 1) * 128], wnat[:, c, :], ident[:, :])
                last.then_inc(w_T, 1)

            def project_qk(hp, c):
                if c == 0:
                    pe.wait_ge(wT_made, hp + 1)
                    pe.wait_ge(xnT_made, 1)
                wait(pe, qkv_rounded, 3 * hp)
                if c and not (isinstance(hp, int) and hp == 0):
                    pe.wait_ge(qkv_rounded, 3 * hp + 1)
                if not isinstance(hp, int):
                    pe.wait_ge(ctxT_made, 2 * B)
                for n in range(2):
                    last = pe.matmul(qkv_home(hp, c)[:, n * 512:(n + 1) * 512], wT[:, c * 128:(c + 1) * 128],
                                     xnT[:, n * 512:(n + 1) * 512], start=True, stop=True)
                last.then_inc(qkv_mm, 1)

            def project_v(hp):
                if not (isinstance(hp, int) and hp == 0):
                    pe.wait_ge(qkv_rounded, 3 * hp + 2)
                if isinstance(hp, int) and hp == 1:
                    pe.wait_ge(ctxT_made, 4)
                for t in range(NT):
                    last = pe.matmul(qkv_home(hp, 2)[:, t * 128:(t + 1) * 128], xnT[:, t * 128:(t + 1) * 128],
                                     wT[:, 256:384], start=True, stop=True)
                last.then_inc(qkv_mm, 1)

            def dots(hp, b):
                s = B * hp + b
                if b == 0:
                    pe.wait_ge(qkv_made, 3 * hp + 2)
                wait(pe, dots_rounded, s)
                for h in range(2):
                    rows = slice(64 * h, 64 * h + 64)
                    for t in range(2):
                        last = pe.matmul(pair[0][:, h * 512 + t * 256:h * 512 + (t + 1) * 256],
                                         qf[rows, b * S + t * 128:b * S + (t + 1) * 128],
                                         kf[rows, b * S:(b + 1) * S], start=True, stop=True)
                last.then_inc(dots_mm, 1)

            def attn_transposes(hp, b):
                s = B * hp + b
                pe.wait_ge(attn_made, s + 1)
                wait(pe, attnT_made, s)
                for h in range(2):
                    for t in range(2):
                        for k in range(2):
                            c = h * 512 + k * 256 + t * 128
                            a = (2 * h + t) * 256 + k * 128
                            last = pe.transpose(pair[1][:, c:c + 128], attn[:, b % 2, a:a + 128], ident[:, :])
                last.then_inc(attn_T, 1)

            def attn_values(hp, b):
                s = B * hp + b
                if b == 0:
                    pe.wait_ge(qkv_made, 3 * hp + 3)
                pe.wait_ge(attnT_made, s + 1)
                wait(pe, o_rounded, s)
                for k in range(2):
                    for h in range(2):
                        last = pe.matmul(pair[3][64 * h:64 * h + 64, 512:768], vf[:, 2 * b + k, 64 * h:64 * h + 64],
                                         attnT[:, h * 512 + k * 256:h * 512 + (k + 1) * 256],
                                         start=(k == 0), stop=(k == 1))
                last.then_inc(pv_mm, 1)

            weights_T(0)
            project_qk(0, 0)
            pe.wait_ge(ctxT_made, 2)
            project_qk(0, 1)
            project_v(0)
            dots(0, 0)
            dots(0, 1)

            def head_pair(hp):
                first, last = (isinstance(hp, int) and hp == end for end in (0, HP - 1))
                for b in range(B):
                    if b == 0 and not last:
                        weights_T(hp + 1)
                    if b == 2 and not last:
                        project_v(hp + 1)
                        attn_values(hp, 1)
                    if b + 2 < B or not last:
                        dots(*batch_of(hp, b, 2))
                    if b < 2 and not last:
                        project_qk(hp + 1, b)
                    if (b or not first) and (b != 2 or last):
                        attn_values(*batch_of(hp, b, -1))
                    attn_transposes(hp, b)
                    if first and b:
                        ctx_transposes(b, (2, 2))

            repeat(pe, HP, head_pair)
            attn_values(HP - 1, B - 1)

            pe.wait_ge(o_made, B * HP)
            for c, tiles in enumerate(OUT_TILES):
                for i, t in enumerate(range(*tiles)):
                    if c and t == NT - 2:
                        xn_transposes(2, pair[1][:, 512:1024], OUT_TILES[0])
                    for n in range(HP):
                        last = pe.matmul(pair[1 - c][:, i * 128:(i + 1) * 128], oT[:, n, t * 128:(t + 1) * 128],
                                         wpT[:, n, :], start=(n == 0), stop=(n == HP - 1))
                last.then_inc(proj_mm, 1)

            def head_of(b, g, j, ahead):
                n = 4 * g + j + ahead
                return (b, n // 4, n % 4) if n < 4 * NG else (b + 1, n // 4 - NG, n % 4)

            def scores(b, g, j, chunks=(0, 1)):
                gi, head, t = NG * b + g, 4 * (g % HG) + j, g // HG
                if j == 0 and t == 0 and 0 in chunks:
                    pe.wait_ge(kq_loaded[g % HG], 96 * (b + 1))
                for c in chunks:
                    k0, size = CHUNKS[c]
                    wait(pe, (half_made, masked_made)[c], 4 * gi + j)
                    for k in range(0, size, 512):
                        w = min(512, size - k)
                        last = pe.matmul(pair[c][:, k:k + w], qstack[0:SROWS, head, t * 128:(t + 1) * 128],
                                         kstack[0:SROWS, head, k0 + k:k0 + k + w], start=True, stop=True)
                    last.then_inc(score_mm, 1)

            def maxima_T(b, g):
                gi = NG * b + g
                pe.wait_ge(nparts_made, gi + 1)
                wait(pe, nm_moved, gi)
                for j in range(4):
                    last = pe.transpose(nm_psum[SHIFT:SHIFT + 3, j * 128:(j + 1) * 128], nparts[:, g % 2, j, :],
                                        identb[:, :])
                last.then_inc(nm_T, 1)

            def tile_scores(b, g, t, masked):
                gi, n, hg, q = NG * b + g, KT * g + t, g % HG, g // HG
                rows = 128 if t < KFULL else KTAIL
                if t == 0:
                    pe.wait_ge(nm_moved, gi + 1)
                    if masked and hg == 0:
                        pe.wait_ge(mparts_made, 2 * b + q + 1)
                wait(pe, expt_made, NG * KT * b + n - 1)
                bank = (n % 2) * 512
                for j in range(4):
                    last = pe.matmul(pair[2][0:rows, bank + j * 128:bank + (j + 1) * 128],
                                     kstack[0:SHIFT + 3, 4 * hg + j, t * 128:t * 128 + rows],
                                     qstack[0:SHIFT + 3, 4 * hg + j, q * 128:(q + 1) * 128],
                                     start=(j == 0), stop=True, skip_group_check=True)
                    if j == 0 and masked:
                        for i in range(3):
                            pe.matmul(pair[2][0:rows, bank:bank + 512].rearrange("k (j q) -> k j q", j=4),
                                      mparts[:, q, i, t * 128:t * 128 + rows],
                                      identb[:, :].unsqueeze(1).broadcast_to([128, 4, 128]),
                                      start=False, stop=True, skip_group_check=True)
                last.then_inc(st_mm, 1)

            def tile_values(b, g, t):
                gi, n, hg = NG * b + g, KT * g + t, g % HG
                rows = 128 if t < KFULL else KTAIL
                if t == 0 and hg == 0:
                    wait(pe, xoT_made, 2 * b + g // HG)
                if t == 0 and g < HG:
                    wait(pe, v_moved, 8 * (b - 1) + min(2 * hg + 4, 8))
                pe.wait_ge(expt_made, NG * KT * b + n + 1)
                for j in range(4):
                    c = VW * (4 * hg + j)
                    last = pe.matmul(pair[3][32 * j:32 * j + 32, hg * 128:(hg + 1) * 128],
                                     v_aug[0:rows, t, c:c + 32],
                                     pT[0:rows, n % 4, j * 128:(j + 1) * 128], start=(t == 0), stop=(t == KT - 1))
                last.then_inc(xpv_mm, 1)

            def finish_tile(b, t, piece):
                u = 2 * b + t
                if piece == 0:
                    pe.wait_ge(xoT_made, u + 1)
                    pe.wait_ge(nm_moved, 4 * u + 4)
                    for g in range(HG):
                        last = pe.transpose(pair[3][:, 512 + g * 128:640 + g * 128], xoT[:, g * 128:(g + 1) * 128], ident[:, :])
                    last.then_inc(xo_T, 1)
                elif piece == 1:
                    pe.wait_ge(cnat_made, u + 1)
                    pe.transpose(pair[3][:, 512:640], cnat, ident[:, :]).then_inc(c_T, 1)
                else:
                    pe.wait_ge(cT_made, u + 1)
                    pe.matmul(pair[3][:, 640:768], cT, woT[:, :], start=True, stop=True).then_inc(xproj_mm, 1)

            pe.wait_ge(x1_made, 2)
            for n in range(AHEAD):
                scores(*head_of(0, 0, 0, n))
                if n == 0:
                    xn_transposes(3, pair[2], OUT_TILES[1])
            maxima_T(0, 0)

            def batch_products(b, masked, last_batch):
                tile_scores(b, 0, 0, masked)
                tile_scores(b, 0, 1, masked)
                for n in range(NG * KT):
                    g, t = n // KT, n % KT
                    finish = g % HG == 0 and not (isinstance(b, int) and b == 0 and g == 0)
                    unit = (b, 0) if g else (b - 1, 1)
                    if n + 2 < NG * KT:
                        tile_scores(b, (n + 2) // KT, (n + 2) % KT, masked)
                    for c in range(2):
                        if t in AHEAD_AT[c] and (not last_batch or 4 * g + AHEAD < 4 * NG):
                            scores(*head_of(b, g, AHEAD_AT[c].index(t), AHEAD), (c,))
                    tile_values(b, g, t)
                    if finish and t in (1, 4, 6):
                        finish_tile(*unit, (1, 4, 6).index(t))
                    if last_batch and (g, t) == (NG - 1, 3):
                        pe.wait_ge(masked_made, 4 * NG * B)
                        xn_transposes(4, pair[0], FFN_TILES[0])
                    if t == maxima_at(finish) and (not last_batch or g + 1 < NG):
                        if finish:
                            pe.wait_ge(xbias_made, 2 * unit[0] + unit[1] + 1)
                        maxima_T(*((b, g + 1) if g + 1 < NG else (b + 1, 0)))

            def batch(b):
                last_batch = isinstance(b, int) and b + 1 == B
                pe.wait_ge(flag_made, b + 1)
                settle(pe, pe_tally, b)
                flag = pe.value_load(mask_flag[0:1, :].bitcast(U32))
                with pe.If(flag != 0):
                    batch_products(b, True, last_batch)
                with pe.Else():
                    batch_products(b, False, last_batch)

            repeat(pe, B, batch)

            def up(m, f, u, c, r):
                if c == 0 and f == 0:
                    pe.wait_ge(wexp_loaded[u], 80 * (r + 1))
                wait(pe, z_made, 2 * m + f - 1)
                for n, w in enumerate((w1_sb, w2_sb)):
                    last = pe.matmul(pair[f][:, n * 512:(n + 1) * 512], w[:, u, f * 128:(f + 1) * 128],
                                     xnT[:, c * 512:(c + 1) * 512], start=True, stop=True)
                last.then_inc(up_mm, 1)

            def gate_linear(m, half, u, c):
                pe.wait_ge(z_made, 2 * m + 2)
                wait(pe, ogl_made, 2 * m + half)
                for n, w in enumerate((wg_sb, wl_sb)):
                    for f in range(2):
                        last = pe.matmul(pair[2][:, n * 512:(n + 1) * 512], w[:, u, f, half * 128:(half + 1) * 128],
                                         zed[:, c, f, :], start=(f == 0), stop=(f == 1))
                last.then_inc(gl_mm, 1)

            def down(m, u, c):
                pe.wait_ge(ogl_made, 2 * m + 2)
                wait(pe, y_added, m - 1)
                for t in range(4):
                    for f in range(2):
                        last = pe.matmul(pair[3][:, c * 512 + t * 128:c * 512 + (t + 1) * 128],
                                         ogl[:, c, f, t * 128:(t + 1) * 128], w3_sb[:, u, f, :],
                                         start=(f == 0), stop=(f == 1))
                last.then_inc(y_mm, 1)

            finish_tile(B - 1, 1, 0)
            pe.wait_ge(xnT_made, 4)
            up(0, 0, 0, 0, 0)
            finish_tile(B - 1, 1, 1)
            finish_tile(B - 1, 1, 2)
            up(0, 1, 0, 0, 0)
            xn_transposes(5, pair[2], FFN_TILES[1])
            pe.wait_ge(xnT_made, 5)
            for t in range(NT):
                last = pe.matmul(pair[3][:, t * NE:(t + 1) * NE], xnT[:, t * 128:(t + 1) * 128], wgate[:, :],
                                 start=True, stop=True)
            last.then_inc(gate_mm, 1)

            def weights_transposes():
                pe.wait_ge(comb_made, 1)
                pe.wait_ge(z_made, 4 * NE - 1)
                for t in range(NT):
                    last = pe.transpose(pair[0][0:NE, t * 128:(t + 1) * 128], comb[:, :, t], ident[:, :])
                last.then_inc(comb_T, 1)

            def down_bias():
                pe.wait_ge(combT_made, 1)
                for t in range(NT):
                    last = pe.matmul(pair[1][:, t * 128:(t + 1) * 128], combT[:, t, :], b3_sb[:, :], start=True, stop=True)
                last.then_inc(b3_mm, 1)

            def two_experts(r):
                more = not isinstance(r, int) or r + 1 < NE // 2
                for u in range(2):
                    for c in range(2):
                        m = 4 * r + 2 * u + c
                        nu, nc_ = (u, 1) if c == 0 else (1 - u, 0)
                        nr = r + 1 if (u, c) == (1, 1) else r
                        final = (u, c) == (1, 1) and not more
                        if final:
                            weights_transposes()
                        for half in range(2):
                            gate_linear(m, half, u, c)
                            if not final:
                                up(m + 1, half, nu, nc_, nr)
                        if final:
                            down_bias()
                        down(m, u, c)

            repeat(pe, NE // 2, two_experts)

        @block.scalar
        def _(act):
            act.wait_ge(wproj_T, 1)
            act.activation(pT[:, 0:2, :].rearrange("p u k -> p (u k)"), pair[3][:, :], ACT.Copy).then_inc(wpT_made, 1)

            def ctx_move(k, pairs):
                for half, size in enumerate((1024, S2 - 1024)):
                    act.wait_ge(ctx_T, 2 * k + half + 1)
                    act.activation(ctxT[:, k, half * 1024:half * 1024 + size], pair[pairs[half]][:, 0:size],
                                   ACT.Copy).then_inc(ctxT_made, 1)

            def std_of(n, tiles=(0, NT)):
                act.wait_ge(var_made, n)
                act.activation(std[:, slice(*tiles)], var_eps[:, slice(*tiles)], ACT.Sqrt).then_inc(std_made, 1)

            def xn_move(n, home, src):
                act.wait_ge(xn_T, n)
                act.activation(home, src, ACT.Copy).then_inc(xnT_made, 1)

            std_of(1)
            ctx_move(0, (0, 1))
            xn_move(1, xnT[:, :], pair[2][:, :])
            act.wait_ge(small_T, 1)
            act.activation(woT[:, :], pair[3][:, 0:128], ACT.Copy).then_inc(smallT_made, 1)
            act.activation(bias_T[:, :], pair[3][:, 128:192], ACT.Copy).then_inc(smallT_made, 1)

            def weights_move(hp):
                act.wait_ge(w_T, hp + 1)
                wait(act, qkv_mm, 3 * hp)
                act.activation(wT[:, :], pair[3][:, 0:384], ACT.Copy).then_inc(wT_made, 1)

            def round_qkv(hp, c):
                act.wait_ge(qkv_mm, 3 * hp + c + 1)
                wait(act, qkv_made, 3 * hp + c - 2)
                act.activation(qkv16[:, c, :], qkv_home(hp, c)[:, :], ACT.Copy, scale=FXP * NUDGE, bias=-0.5).then_inc(qkv_rounded, 1)

            def round_dots(hp, b):
                s = B * hp + b
                act.wait_ge(dots_mm, s + 1)
                wait(act, dots_made, s - 1)
                act.activation(dot16[:, b % 2, :], pair[0][:, :], ACT.Copy,
                               scale=NUDGE * DH ** -0.5 / FXP, bias=-0.5).then_inc(dots_rounded, 1)

            def exps(hp, b):
                s = B * hp + b
                act.wait_ge(dots_made, s + 1)
                wait(act, attn_T, s - 1)
                for k in range(4):
                    last = act.activation(expd[:, b % 2, k * 256:(k + 1) * 256], dotf[:, b % 2, k * 256:(k + 1) * 256],
                                          ACT.Exp, scale=1.0 / FXP, accum_out=esum[:, b % 2, k:k + 1])
                last.then_inc(exp_made, 1)

            def attn_move(hp, b):
                s = B * hp + b
                act.wait_ge(attn_T, s + 1)
                wait(act, pv_mm, s)
                act.activation(attnT, pair[1][:, :], ACT.Copy).then_inc(attnT_made, 1)

            weights_move(0)
            for c in range(3):
                round_qkv(0, c)

            round_dots(0, 0)
            round_dots(0, 1)

            def head_pair(hp):
                first, last = (isinstance(hp, int) and hp == end for end in (0, HP - 1))
                for b in range(B):
                    if b == 0 and not last:
                        weights_move(hp + 1)
                    exps(hp, b)
                    if b or not first:
                        attn_move(*batch_of(hp, b, -1))
                    if b == 2 and not last:
                        round_qkv(hp + 1, 2)
                    if b + 2 < B or not last:
                        round_dots(*batch_of(hp, b, 2))
                    if b < 2 and not last:
                        round_qkv(hp + 1, b)
                    if first and b:
                        ctx_move(b, (2, 2))

            repeat(act, HP, head_pair)
            attn_move(HP - 1, B - 1)
            for c, (tiles, home) in enumerate(zip(OUT_TILES, (pair[1][:, 512:1024], pair[2]))):
                size = 128 * (tiles[1] - tiles[0])
                std_of(2 + c, tiles)
                xn_move(2 + c, xq_T[:, 128 * tiles[0]:128 * tiles[1]], home[:, 0:size])
            later = slice(128 * OUT_TILES[1][0], T)
            for i in range(3):
                act.wait_ge(rest_made if i else xnT_made, i or 3)
                act.activation(qparts[:, i, later], xq_T[:, later], ACT.Copy).then_inc(part_made if i < 2 else qparts_made, 1)
            act.activation(warm[:, :], var_eps[:, 0:1], ACT.Exp)

            def maxima_move(b, g):
                gi, hg, q = NG * b + g, g % HG, g // HG
                act.wait_ge(nm_T, gi + 1)
                act.activation(qstack[SHIFT:SHIFT + 3, 4 * hg:4 * hg + 4, q * 128:(q + 1) * 128],
                               nm_psum[SHIFT:SHIFT + 3, 0:512].rearrange("i (j q) -> i j q", j=4),
                               ACT.Copy).then_inc(nm_moved, 1)

            def tile_exp(b, g, t):
                n = KT * g + t
                rows = 128 if t < KFULL else KTAIL
                act.wait_ge(st_mm, NG * KT * b + n + 1)
                wait(act, xpv_mm, NG * KT * b + n - 3)
                act.activation(pT[0:rows, n % 4, :], pair[2][0:rows, (n % 2) * 512:(n % 2) * 512 + 512],
                               ACT.Exp).then_inc(expt_made, 1)

            def finish_tile(b, t, piece):
                u = 2 * b + t
                if piece == 0:
                    act.wait_ge(xpv_mm, KT * HG * (u + 1))
                    wait(act, xo_T, u)
                    act.activation(xoT, pair[3][:, 0:512], ACT.Copy).then_inc(xoT_made, 1)
                else:
                    act.wait_ge(c_T, u + 1)
                    wait(act, xproj_mm, u)
                    act.activation(cT, pair[3][:, 512:640], ACT.Copy).then_inc(cT_made, 1)

            act.wait_ge(stacks_set, 4)
            maxima_move(0, 0)

            def batch(b):
                last_batch = isinstance(b, int) and b + 1 == B
                for g in range(NG):
                    finish = g % HG == 0 and not (isinstance(b, int) and b == 0 and g == 0)
                    unit = (b, 0) if g else (b - 1, 1)
                    for t in range(KT):
                        tile_exp(b, g, t)
                        if finish and t in (0, 5):
                            finish_tile(*unit, (0, 5).index(t))
                        if last_batch and (g, t) == (NG - 2, 11):
                            std_of(4, FFN_TILES[0])
                        if last_batch and (g, t) == (NG - 1, 5):
                            xn_move(4, xnT[:, 0:128 * FFN_TILES[0][1]], pair[0][:, 0:128 * FFN_TILES[0][1]])
                        if t == maxima_at(finish) + 2 and (not last_batch or g + 1 < NG):
                            maxima_move(*((b, g + 1) if g + 1 < NG else (b + 1, 0)))

            repeat(act, B, batch)

            def up_bias(m, f, e):
                wait(act, z_made, 2 * m + f - 1)
                act.wait_ge(up_mm, 2 * m + f + 1)
                bias = bias_T[:, bass.ds(2 * e + f, 1)]
                settle(act, act_tally, m)
                act.activation(x1s[:, f, :], pair[f][:, 0:512], ACT.Identity,
                               bias=bias).then_inc(x1s_made, 1)

            def gate_silu(m, half, e):
                wait(act, ogl_made, 2 * m + half - 1)
                act.wait_ge(gl_mm, 2 * m + half + 1)
                bias = bias_T[:, bass.ds(32 + 2 * e + half, 1)]
                settle(act, act_tally, m)
                act.activation(silu[:, half, :], pair[2][:, 0:512], ACT.Silu,
                               bias=bias).then_inc(silu_made, 1)

            finish_tile(B - 1, 1, 0)
            act.wait_ge(mparts_made, 2 * B)
            up_bias(0, 0, 0)
            finish_tile(B - 1, 1, 1)
            std_of(5, FFN_TILES[1])
            up_bias(0, 1, 0)
            xn_move(5, xnT[:, 128 * FFN_TILES[1][0]:T], pair[2][:, 0:T - 128 * FFN_TILES[1][0]])
            act.wait_ge(gdiff_made, 1)
            act.activation(gw[:, :, 1], gw[:, :, 0], ACT.Exp).then_inc(gexp_made, 1)

            def two_experts(r):
                more = not isinstance(r, int) or r + 1 < NE // 2
                for u in range(2):
                    for c in range(2):
                        m, e = 4 * r + 2 * u + c, 2 * r + u
                        final = (u, c) == (1, 1) and not more
                        if final:
                            act.wait_ge(comb_T, 1)
                            act.activation(combT[:, :, :].rearrange("e t p -> e (t p)"), pair[0][0:NE, :],
                                           ACT.Copy).then_inc(combT_made, 1)
                        for half in range(2):
                            gate_silu(m, half, e)
                            if not final:
                                up_bias(m + 1, half, e + c)

            repeat(act, NE // 2, two_experts)

        @block.vector
        def _(dve):
            chain = Chain(dve, dve_step)

            def layer_norm(n, src, tiles=(0, NT)):
                for t in range(*tiles):
                    last = dve.bn_stats(stats[:, t, :], src[:, t, :])
                chain.step(last)
                for t in range(*tiles):
                    last = dve.bn_aggr(meanvar[:, t, :], stats[:, t, :])
                chain.step(last)
                cut_ = slice(*tiles)
                dve.tensor_scalar(var_eps[:, cut_], meanvar[:, cut_, 1], LN_EPS, None, ALU.add).then_inc(var_made, 1)
                dve.wait_ge(std_made, n)
                chain.step(dve.reciprocal(rstd[:, cut_], std[:, cut_]))
                for t in range(*tiles):
                    last = dve.tensor_scalar(xn[:, t, :], src[:, t, :], meanvar[:, t, 0:1], rstd[:, t:t + 1],
                                             ALU.subtract, ALU.mult)
                last.then_inc(xn_made, 1)

            def truncate(out_, floor16):
                return dve.scalar_tensor_tensor(out_, floor16, 0.0, floor16, ALU.is_lt, ALU.add)

            dve.wait_ge(x_loaded, 16)
            layer_norm(1, x_in)
            dve.wait_ge(small_loaded, 16 * 10)
            chain.step(dve.tensor_scalar(bproj_fx[:, :], bproj_bc[:, :], FXP * NUDGE, -0.5, ALU.mult, ALU.add))

            def make_qkv(hp, c):
                dve.wait_ge(qkv_rounded, 3 * hp + c + 1)
                if c < 2:
                    wait(dve, dots_mm, B * hp)
                else:
                    wait(dve, pv_mm, B * hp)
                home = (qf, kf, vf)[c]
                src = qkv16[:, c, :] if c < 2 else qkv16[:, c, :].rearrange("p (t e) -> p t e", t=NT)
                truncate(home, src).then_inc(qkv_made, 1)

            def make_dots(hp, b):
                s = B * hp + b
                dve.wait_ge(dots_rounded, s + 1)
                wait(dve, exp_made, s - 1)
                truncate(dotf[:, b % 2, :], dot16[:, b % 2, :]).then_inc(dots_made, 1)

            def make_attn(hp, b):
                s = B * hp + b
                dve.wait_ge(exp_made, s + 1)
                chain.step(dve.tensor_scalar(esum4k[:, :], esum[:, b % 2, :], 1.0 / (FXP * NUDGE), None, ALU.mult))
                chain.step(dve.reciprocal(rnorm[:, :], esum4k[:, :]))
                for k in range(4):
                    last = dve.tensor_scalar(attn_h[:, b % 2, k * 256:(k + 1) * 256], expd[:, b % 2, k * 256:(k + 1) * 256],
                                             rnorm[:, k:k + 1], -0.5, ALU.mult, ALU.add)
                chain.step(last)
                dve.tensor_scalar(attn[:, b % 2, :], attn_h[:, b % 2, :], MAGIC, MAGIC, ALU.add,
                                  ALU.subtract).then_inc(attn_made, 1)

            def make_o(hp, b):
                s = B * hp + b
                wait(dve, o_made, s)
                dve.wait_ge(pv_mm, s + 1)
                dve.tensor_scalar(o16[:, :], pair[3][:, 512:768], NUDGE / FXP, -0.5, ALU.mult, ALU.add).then_inc(o_rounded, 1)
                dve.wait_ge(o_rounded, s + 1)
                home = oT[:, hp, b * S:(b + 1) * S] if isinstance(hp, int) else \
                    region_g[:, bass.ds(hp * T + b * S, S)]
                truncate(home, o16[:, :]).then_inc(o_made, 1)

            for c in range(3):
                make_qkv(0, c)
            make_dots(0, 0)
            start, steps = chain.base + chain.n, 3 * B

            def head_pair(hp):
                chain.repetition(start, hp, steps)
                first, last = (isinstance(hp, int) and hp == end for end in (0, HP - 1))
                for b in range(B):
                    if b + 1 < B or not last:
                        make_dots(*batch_of(hp, b, 1))
                    make_attn(hp, b)
                    if b == 1 and not last:
                        make_qkv(hp + 1, 0)
                    if b or not first:
                        make_o(*batch_of(hp, b, -1))
                    if b == 1 and not last:
                        make_qkv(hp + 1, 1)
                    if b == 0 and not first:
                        make_qkv(hp, 2)

            repeat(dve, HP, head_pair)
            chain.after(start, HP, steps)
            make_o(HP - 1, B - 1)

            def mask_largest(b, t, piece):
                if piece == 0:
                    dve.wait_ge(mask_loaded[t], 16 * (b + 1))
                quarter, column = slice(piece * S2 // 4, (piece + 1) * S2 // 4), 4 * t + piece
                last = dve.tensor_reduce(mask_hi[:, column:column + 1], mask_sb[:, t, quarter], AX.X, ALU.max,
                                         apply_absolute_value=True)
                if column == 7:
                    chain.step(last)
                    wait(dve, flag_made, b)
                    dve.tensor_reduce(mask_any[:, :], mask_hi[:, :], AX.X, ALU.max,
                                      apply_absolute_value=True).then_inc(any_made, 1)

            def attention_out(c):
                tiles = slice(*OUT_TILES[c])
                tokens = slice(128 * tiles.start, 128 * tiles.stop)
                count, size = tiles.stop - tiles.start, tokens.stop - tokens.start
                floor16 = qkv16[:, 0, tokens].rearrange("p (t d) -> p t d", t=count)
                dve.wait_ge(proj_mm, c + 1)
                chain.step(dve.scalar_tensor_tensor(floor16, pair[1 - c][:, 0:size].rearrange("p (t d) -> p t d", t=count),
                                                    NUDGE, bproj_fx[:, :].unsqueeze(1).broadcast_to([128, count, D]),
                                                    ALU.mult, ALU.add))
                chain.step(truncate(xn[:, tiles, :], floor16))
                dve.scalar_tensor_tensor(x1[:, tiles, :], xn[:, tiles, :], 1.0 / FXP, x_in[:, tiles, :], ALU.mult,
                                         ALU.add).then_inc(x1_made, 1)
                dve.wait_ge(x1_made, c + 1)
                layer_norm(2 + c, x1, OUT_TILES[c])
                if c:
                    return
                dve.wait_ge(xnT_made, 2)
                for i in range(3):
                    if i < 2:
                        chain.step(dve.tensor_copy(qparts[:, i, tokens], xq_T[:, tokens]))
                        chain.step(dve.tensor_tensor(xq_T[:, tokens], xq_T[:, tokens], qparts[:, i, tokens], ALU.subtract))
                    else:
                        dve.tensor_copy(qparts[:, i, tokens], xq_T[:, tokens]).then_inc(qparts_made, 1)

            for column in range(8):
                mask_largest(0, column // 4, column % 4)
            for c in range(2):
                attention_out(c)

            def row_maximum(b, g, j, c):
                gi, t = NG * b + g, g // HG
                k0, size = CHUNKS[c]
                if c == 0:
                    if j == 0 and g % HG == 0:
                        dve.wait_ge(mask_loaded[t], 16 * (b + 1))
                    wait(dve, half_made, 4 * gi + j)
                    wait(dve, nparts_made, gi - 1)
                    first = 3.0e38
                else:
                    wait(dve, masked_made, 4 * gi + j)
                    dve.wait_ge(half_made, 4 * gi + j + 1)
                    first = nmax[:, g % 2, j, 0:1]
                dve.wait_ge(score_mm, 8 * gi + 2 * j + c + 1)
                settle(dve, dve_tally, b)
                dve.tensor_tensor_reduce(out=unused[c][:, 0:size], in0=pair[c][:, 0:size],
                                         in1=mask_sb[:, t, k0:k0 + size], scale=-1.0, scalar=first,
                                         op0=ALU.add, op1=ALU.min,
                                         accum_out=nmax[:, g % 2, j, c:c + 1]).then_inc((half_made, masked_made)[c], 1)

            def split_maxima(b, g, step):
                gi = NG * b + g
                if step == 0:
                    dve.wait_ge(masked_made, 4 * gi + 4)
                    wait(dve, nm_T, gi - 1)
                else:
                    chain.join()
                src = nmax[:, g % 2, :, 1] if step < 2 else nrest[:, :]
                part = nparts[:, g % 2, :, step // 2]
                if step == 4:
                    dve.tensor_copy(part, src).then_inc(nparts_made, 1)
                elif step % 2 == 0:
                    chain.later(dve.tensor_copy(part, src))
                else:
                    chain.later(dve.tensor_tensor(nrest[:, :], src, part, ALU.subtract))

            def finish_tile(b, t, piece):
                u = 2 * b + t
                if piece == 0:
                    dve.wait_ge(xo_T, u + 1)
                    heads = pair[3][:, 512:1024].rearrange("p (h c) -> p h c", h=H)
                    chain.step(dve.reciprocal(rsum_x[:, :], heads[:, :, XD]))
                    wait(dve, c_T, u)
                    dve.tensor_tensor(cnat.rearrange("p (h c) -> p h c", h=H), heads[:, :, 0:XD],
                                      rsum_x[:, :].unsqueeze(2).broadcast_to([128, H, XD]), ALU.mult).then_inc(cnat_made, 1)
                else:
                    dve.wait_ge(xproj_mm, u + 1)
                    wait(dve, x2_made, u)
                    dve.tensor_tensor(xo[:, :], pair[3][:, 640:768], wob_bc[:, :], ALU.add).then_inc(xbias_made, 1)
                    dve.wait_ge(xbias_made, u + 1)
                    tile = slice(u, u + 1) if isinstance(u, int) else bass.ds(u, 1)
                    dve.scalar_tensor_tensor(acc[:, tile, :], xo[:, :].unsqueeze(1), 0.0, x1[:, tile, :], ALU.max,
                                             ALU.add).then_inc(x2_made, 1)

            def head_of(b, g, j, ahead):
                n = 4 * g + j + ahead
                return (b, n // 4, n % 4) if n < 4 * NG else (b + 1, n // 4 - NG, n % 4)

            for n in range(AHEAD):
                for c in range(2):
                    row_maximum(*head_of(0, 0, 0, n), c)
                if n in (1, 3):
                    i, later = n // 2, slice(128 * OUT_TILES[1][0], T)
                    dve.wait_ge(part_made, i + 1)
                    dve.tensor_tensor(xq_T[:, later], xq_T[:, later], qparts[:, i, later], ALU.subtract).then_inc(rest_made, 1)
                if n == 3:
                    for step in range(5):
                        split_maxima(0, 0, step)
            start, steps = chain.base + chain.n, NG * 4 + 2 + 1

            def batch(b):
                chain.repetition(start, b, steps)
                last_batch = isinstance(b, int) and b + 1 == B
                for g in range(NG):
                    finish = g % HG == 0 and not (isinstance(b, int) and b == 0 and g == 0)
                    unit = (b, 0) if g else (b - 1, 1)
                    ahead = not last_batch or 4 * g + AHEAD < 4 * NG
                    split = not last_batch or g + 1 < NG
                    for j in range(4):
                        if finish and j in (0, 2):
                            finish_tile(*unit, j // 2)
                        for c in range(2):
                            if split and 2 * j + c < 5:
                                split_maxima(*((b, g + 1) if g + 1 < NG else (b + 1, 0)), 2 * j + c)
                            if ahead:
                                row_maximum(*head_of(b, g, j, AHEAD), c)
                        if not last_batch and (g, j) in MASK_AT:
                            piece = MASK_AT.index((g, j))
                            mask_largest(b + 1, piece // 4, piece % 4)
                    if last_batch and g == NG - 2:
                        dve.wait_ge(x2_made, FFN_TILES[0][1])
                        layer_norm(4, acc, FFN_TILES[0])
                if isinstance(b, int) and b == 0:
                    chain.n += 1
                    dve.sem_inc(dve_step, 1)
                if last_batch:
                    chain.n += 4 + 1 - 3
                    dve.sem_inc(dve_step, 4 + 1 - 3)

            repeat(dve, B, batch)
            chain.after(start, B, steps)
            def zed_of(m, f, e, c):
                dve.wait_ge(x1s_made, 2 * m + f + 1)
                wait(dve, gl_mm, 2 * m - 2)
                dve.scalar_tensor_tensor(zed[:, c, f, :], pair[f][:, 512:1024], bias_T[:, bass.ds(16 + 2 * e + f, 1)],
                                         x1s[:, f, :], ALU.add, ALU.mult).then_inc(z_made, 1)

            def ogl_of(m, half, e, c):
                dve.wait_ge(silu_made, 2 * m + half + 1)
                wait(dve, y_mm, m - 1)
                dve.scalar_tensor_tensor(ogl[:, c, half, :], pair[2][:, 512:1024], bias_T[:, bass.ds(48 + 2 * e + half, 1)],
                                         silu[:, half, :], ALU.add, ALU.mult).then_inc(ogl_made, 1)

            def add_expert(m, e, c):
                dve.wait_ge(y_mm, m + 1)
                wait(dve, y_added, m - 1)
                weight = comb[:, :, :].rearrange("p e t -> p (e t)")
                for t in range(4):
                    last = dve.scalar_tensor_tensor(acc[:, 4 * c + t, :], pair[3][:, c * 512 + t * 128:c * 512 + (t + 1) * 128],
                                                    weight[:, bass.ds(e * NT + 4 * c + t, 1)], acc[:, 4 * c + t, :],
                                                    ALU.mult, ALU.add)
                last.then_inc(y_added, 1)

            finish_tile(B - 1, 1, 0)
            zed_of(0, 0, 0, 0)
            finish_tile(B - 1, 1, 1)
            dve.wait_ge(x2_made, 2 * B)
            layer_norm(5, acc, FFN_TILES[1])
            zed_of(0, 1, 0, 0)
            dve.wait_ge(gate_mm, 1)
            chain.step(dve.tensor_tensor(gate[:, :, :], pair[3][:, 0:NT * NE].rearrange("p (t e) -> p t e", t=NT),
                                         bgate_bc[:, :].unsqueeze(1).broadcast_to([128, NT, NE]), ALU.add))
            for t in range(NT):
                last = dve.max(gtop[:, t, :], gate[:, t, :])
            chain.step(last)
            dve.tensor_tensor(gw[:, :, 0], gtop[:, :, 1], gtop[:, :, 0], ALU.subtract).then_inc(gdiff_made, 1)
            for t in range(NT):
                last = dve.max_index(gidx[:, t, :], gtop[:, t, :], gate[:, t, :])
            chain.step(last)
            chain.step(dve.tensor_copy(gidf[:, :, :], gidx[:, :, :]))
            dve.wait_ge(gexp_made, 1)
            chain.step(dve.tensor_scalar(gw[:, :, 2], gw[:, :, 1], 1.0, None, ALU.add))
            chain.step(dve.reciprocal(gw[:, :, 3], gw[:, :, 2]))
            chain.step(dve.tensor_tensor(gw[:, :, 2], gw[:, :, 1], gw[:, :, 3], ALU.mult))
            dve.wait_ge(iota_made, 1)
            every = [128, NT, NE]
            for k in range(2):
                last = dve.tensor_tensor(pick[:, k, :, :], iota_e[:, :].unsqueeze(1).broadcast_to(every),
                                         gidf[:, :, k:k + 1].broadcast_to(every), ALU.is_equal)
            chain.step(last)
            for k in range(2):
                last = dve.tensor_tensor(pick[:, k, :, :], pick[:, k, :, :],
                                         gw[:, :, 3 - k:4 - k].broadcast_to(every), ALU.mult)
            chain.step(last)
            dve.tensor_tensor(comb[:, :, :].rearrange("p e t -> p t e"), pick[:, 0, :, :], pick[:, 1, :, :],
                              ALU.add).then_inc(comb_made, 1)

            def two_experts(r):
                more = not isinstance(r, int) or r + 1 < NE // 2
                for u in range(2):
                    for c in range(2):
                        m, e = 4 * r + 2 * u + c, 2 * r + u
                        final = (u, c) == (1, 1) and not more
                        for half in range(2):
                            ogl_of(m, half, e, c)
                            if not final:
                                zed_of(m + 1, half, e + c, 1 - c)
                        if final:
                            dve.wait_ge(b3_mm, 1)
                            dve.wait_ge(y_added, 2 * NE - 1)
                            dve.tensor_tensor(acc[:, :, :], acc[:, :, :], pair[1][:, :].rearrange("p (t d) -> p t d", t=NT),
                                              ALU.add).then_inc(acc_made, 1)
                            dve.wait_ge(acc_made, 1)
                        add_expert(m, e, c)

            repeat(dve, NE // 2, two_experts)


_INS = ['x', 'ctx_1024', 'mask_Bx1xSxS2_ff0', 'L0_attn_w_qkv', 'L0_attn_w_proj', 'L0_attn_b_proj',
        'L0_xattn_wo_w', 'L0_xattn_wo_b', 'L0_ffn_Wgate', 'L0_ffn_bgate', 'L0_ffn_W1', 'L0_ffn_b1',
        'L0_ffn_W2', 'L0_ffn_b2', 'L0_ffn_Wg', 'L0_ffn_bg', 'L0_ffn_Wl', 'L0_ffn_bl', 'L0_ffn_W3', 'L0_ffn_b3']


def kernel(**inputs):
    import numpy as _np
    import concourse.bacc as _bacc
    from concourse import mybir as _mybir
    from concourse.bass_utils import run_bass_kernel_spmd as _run

    nc = _bacc.Bacc("TRN2", target_bir_lowering=False, num_devices=1)
    arrays, args = {}, []
    for name in _INS:
        a = _np.ascontiguousarray(inputs[name])
        arrays[f"in_{name}"] = a
        args.append(nc.dram_tensor(f"in_{name}", a.shape, _mybir.dt.from_np(a.dtype), kind="ExternalInput").ap())
    out = nc.dram_tensor("out", (4, 256, 128), _mybir.dt.float32, kind="ExternalOutput").ap()
    decoder_layer(nc, *args, out)
    r = _run(nc, [arrays], core_ids=[0])
    return r.results[0]["out"]
```
